# Optimizing a Trainium2 kernel written in Bass

```python
import numpy as np
import jax
import jax.numpy as jnp

def _softmax(x, axis=-1):
    return jax.nn.softmax(x, axis=axis)

def _gelu(x):
    return jax.nn.gelu(x, approximate=True)

def _silu(x):
    return jax.nn.silu(x)

def _sigmoid(x):
    return jax.nn.sigmoid(x)

def _layernorm(x, axis=-1, eps=1e-05):
    m = jnp.mean(x, axis=axis, keepdims=True)
    v = jnp.var(x, axis=axis, keepdims=True)
    return (x - m) / jnp.sqrt(v + eps)

def _scatter_add(tgt, idx, src, axis=0):
    return tgt.at[idx].add(src)

def _segment_sum(src, seg, n):
    return jax.ops.segment_sum(src, seg, n)
kernel_name = 'mk_seq_postln_d1_jaxref_r8_12d7a5'

def setup_inputs(seed: int=0):
    np.random.seed(seed)
    _w = jnp.asarray

    def _L0_attn_setup():
        import jax, jax.numpy as jnp
        import numpy as np
        B, L, D_MODEL, NH = (1, 256, 128, 8)
        H = D_MODEL // NH
        SCALE = 0.02
        key = jax.random.key(seed)
        ks = jax.random.split(key, 13)
        d = D_MODEL
        return {'u': jax.random.normal(ks[0], (B, L, d), dtype=jnp.float32), 'Wq': jax.random.normal(ks[1], (d, d), dtype=jnp.float32) * SCALE, 'bq': jax.random.normal(ks[2], (d,), dtype=jnp.float32) * SCALE, 'Wk': jax.random.normal(ks[3], (d, d), dtype=jnp.float32) * SCALE, 'bk': jax.random.normal(ks[4], (d,), dtype=jnp.float32) * SCALE, 'Wv': jax.random.normal(ks[5], (d, d), dtype=jnp.float32) * SCALE, 'bv': jax.random.normal(ks[6], (d,), dtype=jnp.float32) * SCALE, 'ssm_k_kernel': jax.random.normal(ks[7], (d, L), dtype=jnp.float32) * SCALE, 'ssm_k_D': jax.random.normal(ks[8], (d,), dtype=jnp.float32), 'ssm_kernel': jax.random.normal(ks[9], (H, L), dtype=jnp.float32) * SCALE, 'D': jax.random.normal(ks[10], (H,), dtype=jnp.float32), 'Wo': jax.random.normal(ks[11], (d, d), dtype=jnp.float32) * SCALE, 'bo': jax.random.normal(ks[12], (d,), dtype=jnp.float32) * SCALE}
    _L0_attn_in = _L0_attn_setup()

    def _L0_ffn_setup():
        import jax, jax.numpy as jnp
        import numpy as np
        D_IN, D_HID = (128, 512)

        def _ternary(key, shape):
            return jax.random.randint(key, shape, -1, 2).astype(jnp.float32)

        def _tlin(x, w, s):
            return jnp.einsum('bsi,oi->bso', x, w) * s
        key = jax.random.key(seed)
        ks = jax.random.split(key, 12)
        inv = lambda fan: 1.0 / np.sqrt(fan).astype(np.float32)
        return {'x': jax.random.normal(ks[0], (4, 256, D_IN), dtype=jnp.float32), 'w1_w': _ternary(ks[1], (D_HID, D_IN)), 'w1_s': jax.random.uniform(ks[2], (D_HID,), dtype=jnp.float32) * inv(D_IN), 'w2_w': _ternary(ks[3], (D_HID, D_IN)), 'w2_s': jax.random.uniform(ks[4], (D_HID,), dtype=jnp.float32) * inv(D_IN), 'h1_w': _ternary(ks[5], (D_HID, D_HID)), 'h1_s': jax.random.uniform(ks[6], (D_HID,), dtype=jnp.float32) * inv(D_HID), 'h2_w': _ternary(ks[7], (D_HID, D_HID)), 'h2_s': jax.random.uniform(ks[8], (D_HID,), dtype=jnp.float32) * inv(D_HID), 'w3_w': _ternary(ks[9], (D_IN, D_HID)), 'w3_s': jax.random.uniform(ks[10], (D_IN,), dtype=jnp.float32) * inv(D_HID)}
    _L0_ffn_in = _L0_ffn_setup()
    _d = {'L0_attn_u': _L0_attn_in['u'], 'L0_attn_Wq': _L0_attn_in['Wq'], 'L0_attn_bq': _L0_attn_in['bq'], 'L0_attn_Wk': _L0_attn_in['Wk'], 'L0_attn_bk': _L0_attn_in['bk'], 'L0_attn_Wv': _L0_attn_in['Wv'], 'L0_attn_bv': _L0_attn_in['bv'], 'L0_attn_ssm_k_kernel': _L0_attn_in['ssm_k_kernel'], 'L0_attn_ssm_k_D': _L0_attn_in['ssm_k_D'], 'L0_attn_ssm_kernel': _L0_attn_in['ssm_kernel'], 'L0_attn_D': _L0_attn_in['D'], 'L0_attn_Wo': _L0_attn_in['Wo'], 'L0_attn_bo': _L0_attn_in['bo'], 'L0_ffn_w1_w': _L0_ffn_in['w1_w'], 'L0_ffn_w1_s': _L0_ffn_in['w1_s'], 'L0_ffn_w2_w': _L0_ffn_in['w2_w'], 'L0_ffn_w2_s': _L0_ffn_in['w2_s'], 'L0_ffn_h1_w': _L0_ffn_in['h1_w'], 'L0_ffn_h1_s': _L0_ffn_in['h1_s'], 'L0_ffn_h2_w': _L0_ffn_in['h2_w'], 'L0_ffn_h2_s': _L0_ffn_in['h2_s'], 'L0_ffn_w3_w': _L0_ffn_in['w3_w'], 'L0_ffn_w3_s': _L0_ffn_in['w3_s']}
    _x0 = _d['L0_attn_u']
    _d['L0_attn_u'] = jax.random.normal(jax.random.fold_in(jax.random.key(seed), 1), (8, 256, 128), dtype=_x0.dtype)
    del _x0
    return _d

def reference(L0_attn_u, L0_attn_Wq, L0_attn_bq, L0_attn_Wk, L0_attn_bk, L0_attn_Wv, L0_attn_bv, L0_attn_ssm_k_kernel, L0_attn_ssm_k_D, L0_attn_ssm_kernel, L0_attn_D, L0_attn_Wo, L0_attn_bo, L0_ffn_w1_w, L0_ffn_w1_s, L0_ffn_w2_w, L0_ffn_w2_s, L0_ffn_h1_w, L0_ffn_h1_s, L0_ffn_h2_w, L0_ffn_h2_s, L0_ffn_w3_w, L0_ffn_w3_s):

    def _L0_attn_ref(u, Wq, bq, Wk, bk, Wv, bv, ssm_k_kernel, ssm_k_D, ssm_kernel, D, Wo, bo):
        import jax, jax.numpy as jnp
        import numpy as np
        B, L, D_MODEL, NH = (1, 256, 128, 8)
        H = D_MODEL // NH
        SCALE = 0.02
        b, l, d = u.shape
        nh = NH
        h = d // nh
        n = 2 * l
        q = jnp.einsum('bld,ed->bel', u, Wq) + bq[None, :, None]
        k = jnp.einsum('bld,ed->bel', u, Wk) + bk[None, :, None]
        v = jnp.einsum('bld,ed->bel', u, Wv) + bv[None, :, None]
        kk_f = jnp.fft.rfft(ssm_k_kernel, n=n, axis=-1)
        k_f = jnp.fft.rfft(k, n=n, axis=-1)
        shift_k = jnp.fft.irfft(kk_f * k_f, n=n, axis=-1)[..., :l]
        k = shift_k + ssm_k_D[:, None] * k
        kq = k.reshape(b, h, nh, l).transpose(0, 2, 1, 3)[:, :, None]
        vv = v.reshape(b, h, nh, l).transpose(0, 2, 1, 3)[:, None]
        kv = kq * vv
        kern_f = jnp.fft.rfft(ssm_kernel, n=n, axis=-1)
        y = jnp.fft.irfft(jnp.fft.rfft(kv, n=n, axis=-1) * kern_f, n=n, axis=-1)[..., :l]
        y = y + kv * D[:, None]
        q5 = q.reshape(b, h, nh, l).transpose(0, 2, 1, 3)[:, :, None]
        y = (q5 * y).sum(axis=1)
        y = y.reshape(b, d, l)
        y = y.transpose(0, 2, 1)
        return y @ Wo.T + bo

    def _L0_ffn_ref(x, w1_w, w1_s, w2_w, w2_s, h1_w, h1_s, h2_w, h2_s, w3_w, w3_s):
        import jax, jax.numpy as jnp
        import numpy as np
        D_IN, D_HID = (128, 512)

        def _ternary(key, shape):
            return jax.random.randint(key, shape, -1, 2).astype(jnp.float32)

        def _tlin(x, w, s):
            return jnp.einsum('bsi,oi->bso', x, w) * s
        h = jax.nn.silu(_tlin(x, w1_w, w1_s)) * _tlin(x, w2_w, w2_s)
        h = jax.nn.gelu(_tlin(h, h1_w, h1_s), approximate=False)
        h = jax.nn.gelu(_tlin(h, h2_w, h2_s), approximate=False)
        return _tlin(h, w3_w, w3_s)
    x = L0_attn_u
    x = _layernorm(x + _L0_attn_ref(x, L0_attn_Wq, L0_attn_bq, L0_attn_Wk, L0_attn_bk, L0_attn_Wv, L0_attn_bv, L0_attn_ssm_k_kernel, L0_attn_ssm_k_D, L0_attn_ssm_kernel, L0_attn_D, L0_attn_Wo, L0_attn_bo), axis=-1)
    x = _layernorm(x + _L0_ffn_ref(x, L0_ffn_w1_w, L0_ffn_w1_s, L0_ffn_w2_w, L0_ffn_w2_s, L0_ffn_h1_w, L0_ffn_h1_s, L0_ffn_h2_w, L0_ffn_h2_s, L0_ffn_w3_w, L0_ffn_w3_s), axis=-1)
    return x

_drawn_inputs = setup_inputs


def setup_inputs(seed=0):
    import zlib

    import numpy as np

    out = dict(_drawn_inputs(seed))
    spreads = {}
    factors = {'L0_attn_Wq': 8.0,
     'L0_attn_bq': 8.0,
     'L0_attn_Wk': 8.0,
     'L0_attn_bk': 8.0,
     'L0_attn_Wv': 8.0,
     'L0_attn_bv': 8.0,
     'L0_attn_ssm_k_kernel': 8.0,
     'L0_attn_ssm_k_D': 8.0,
     'L0_attn_ssm_kernel': 8.0,
     'L0_attn_D': 7.179,
     'L0_attn_Wo': 8.0,
     'L0_attn_bo': 3.028,
     'L0_ffn_w1_w': 8.0,
     'L0_ffn_w1_s': 8.0,
     'L0_ffn_w2_w': 8.0,
     'L0_ffn_w2_s': 8.0,
     'L0_ffn_h1_w': 8.0,
     'L0_ffn_h1_s': 8.0,
     'L0_ffn_h2_w': 8.0,
     'L0_ffn_h2_s': 8.0,
     'L0_ffn_w3_w': 8.0,
     'L0_ffn_w3_s': 8.0}
    for name, (base, spread) in spreads.items():
        noise = np.random.default_rng([zlib.crc32(name.encode()), seed]).standard_normal(out[name].shape)
        drawn = base * np.exp(spread * noise) if base else spread * noise
        out[name] = jnp.asarray(drawn.astype(out[name].dtype))
    for name, factor in factors.items():
        out[name] = (out[name] * factor).astype(out[name].dtype)
    return out
```

```python
from contextlib import ExitStack

import concourse.bass as bass
from concourse import mybir

F32 = mybir.dt.float32
F32R = mybir.dt.float32r
BF16 = mybir.dt.bfloat16
I32 = mybir.dt.int32
ALU = mybir.AluOpType
ACT = mybir.ActivationFunctionType

P = 128
BATCH, L, D = 8, 256, 128
NH = 8
H = D // NH
G, B, LB = 2, 4, L // P
TPG = LB * B
TILES = G * TPG
CHUNKS, CT = G * LB, B
CW = CT * P
HID = 512
KB = HID // P
EPS = 1e-5
SEG = 1408
FB = 2


def step_order():
    head = lambda g, h: ("head", g, h)
    first = [("spec",)] + [("qkv", 0, t) for t in range(TPG)] + [("fwd", 0, 0), ("fwd", 0, 1)]
    first += [("toeplitz",)] + [("qkv", 1, t) for t in range(TPG)] + [("inv", 0, 0), ("inv", 0, 1)]
    first += [("kv0", 0), ("fwd", 1, 0), head(0, 0), head(0, 1), ("fwd", 1, 1)]
    first += [head(0, h) for h in range(2, 7)] + [("weights",), ("inv", 1, 0), ("inv", 1, 1)]
    first += [head(0, h) for h in range(7, H)] + [("kv0", 1), ("ytr", 0), ("ytr", 1), head(1, 0), ("wo", 0)]
    first += [head(1, 1), ("wo", 1), ("wtest",), head(1, 2), head(1, 3), ("x1tr", 0), head(1, 4), ("x1tr", 1)]

    def ffn(g):
        a, b = 2 * g, 2 * g + 1
        out = [("up", c, ob) for c in (a, b) for ob in range(KB)]
        out += [("hid", layer, c, ob) for layer in (1, 2) for c in (a, b) for ob in range(KB)]
        return out + [("down", a), ("down", b), ("ztr", a), ("ztr", b)]

    rest = [head(1, h) for h in range(5, H)]
    rest += [("ytr", 2), ("ytr", 3), ("wo", 2), ("wo", 3), ("gap",), ("gap",), ("x1tr", 2), ("x1tr", 3)]
    merged = []
    for i, item in enumerate(ffn(0)):
        merged.append(item)
        if rest:
            merged.append(rest.pop(0))
    return first + merged + rest + ffn(1) + [("end",)]


def banks_of(steps):
    at, used, last, turn = {}, [0] * 8, [None] * 8, {}

    def take(key, pool):
        n = turn.get(pool, 0)
        turn[pool] = n + 1
        bank = pool[n % len(pool)]
        at[key] = (bank, used[bank], last[bank])
        used[bank] += 1
        last[bank] = key

    front, side, every = (0, 1, 2, 3), (4, 5, 6, 7), tuple(range(8))
    heads_done = False
    for s in steps:
        late = every if heads_done else side
        if s[0] == "spec" or s[0] in ("qkv", "inv"):
            take(s, side)
        elif s[0] == "fwd":
            take(s + ("re",), front)
            take(s + ("im",), front)
        elif s[0] == "head":
            take(s, front)
            heads_done = s == ("head", 1, H - 1)
        elif s[0] == "up":
            take(s + (1,), late)
            take(s + (2,), late)
        elif s[0] == "wtest":
            take(s, side)
        elif s[0] in ("ytr", "wo", "x1tr", "hid", "down", "ztr"):
            take(s, late)
    return at


def build(nc, a):
    steps = step_order()
    bank = banks_of(steps)
    blocks = [(0,) + s[1:] if s[0] == "up" else s[1:] for s in steps if s[0] in ("up", "hid")]
    place = {b: n for n, b in enumerate(blocks)}
    layers = sorted({b[:2] for b in blocks}, key=lambda lc: place[lc + (0,)])
    hidden_no = {lc: n for n, lc in enumerate(layers)}
    RING = 4

    with ExitStack() as ctx:
        def sb(name, shape, dt=F32):
            return ctx.enter_context(nc.sbuf_tensor(name, shape, dt))

        def sem(name):
            return ctx.enter_context(nc.semaphore(name))

        tok = sb("tok", [P, TILES, 3, P])
        early = ctx.enter_context(ExitStack())

        def esb(name, shape, dt=F32):
            return early.enter_context(nc.sbuf_tensor(name, shape, dt))

        xT = esb("xT", [P, TILES, P])
        dft = esb("dft", [P, LB, 4 * P])
        idft = esb("idft", [P, 2 * FB, L])
        kkT = esb("kkT", [P, LB, P])
        spec_a, spec_b = esb("spec_a", [P, FB, P]), esb("spec_b", [P, FB, P])
        spec_c, spec_t = esb("spec_c", [P, P]), esb("spec_t", [P, P])
        prod = esb("prod", [P, FB, 4, CW])
        ys = esb("ys", [P, 2 * FB, CW])
        wdiff = esb("wdiff", [P, SEG], BF16)
        early.close()
        hidden = sb("hidden", [P, 3, 2, KB, CW], F32R)

        k2 = sb("k2", [P, G, TPG, P])
        toep = sb("toep", [P, H, L])
        kv = sb("kv", [P, 3, TPG, NH, NH])
        prd = sb("prd", [P, TPG, NH, H, NH])
        yT = sb("yT", [P, LB, CW])
        x1T = sb("x1T", [P, 2, LB, CW], F32R)
        NW = (2 + 2 * KB) * HID + KB * P
        w = sb("w", [P, NW])
        wr = sb("wr", [P, NW], F32R)
        ring = sb("ring", [P, RING, CW])
        z = sb("z", [P, CW])
        ident = sb("ident", [P, P])
        wqkv = sb("wqkv", [P, 3 * P])
        bqkv = sb("bqkv", [P, 3 * P])
        woT = sb("woT", [P, P])
        bo = sb("bo", [P, P])
        dcol = sb("dcol", [P, H])
        kd = sb("kd", [1, P])
        mask = sb("mask", [P, 2])
        scales = sb("scales", [P, 4, KB])
        s3 = sb("s3", [P, 1])
        ones = sb("ones", [P, 1])
        halves = sb("halves", [P, CT])
        stats = sb("stats", [P, 2, CHUNKS, CT, nc.vector.BN_STATS_DIM])
        mv = sb("mv", [P, 2, CHUNKS, CT, nc.vector.BN_AGGR_DIM])
        rstd = sb("rstd", [P, 2, CHUNKS, 2, CT])
        wsum = sb("wsum", [P, NW // SEG])
        wflag = sb("wflag", [1, NW // SEG + 1])
        psum = ctx.enter_context(nc.psum_tensor("psum", [P, 8, 512], F32))

        def w_of(t, which, k, ob):
            if which < 2:
                lo = which * HID + ob * P
            elif which < 4:
                lo = (2 + (which - 2) * KB + k) * HID + ob * P
            else:
                lo = (2 + 2 * KB) * HID + k * P
            return t[:, lo:lo + P]

        loads = ["kk", "dft", "wqkv", "xT0", "xT1", "idft", "toep", "small", "w", "x0", "x1"]
        loaded = {n: sem(f"loaded_{n}") for n in loads}
        bank_full = [sem(f"bank_full{i}") for i in range(8)]
        const_ready = sem("const_ready")
        kk_ready = sem("kk_ready")
        spec_ready = sem("spec_ready")
        qkv_ready = sem("qkv_ready")
        prod_ready = sem("prod_ready")
        ys_ready = sem("ys_ready")
        k2_ready = sem("k2_ready")
        toep_ready = sem("toep_ready")
        kv_ready = sem("kv_ready")
        prd_ready = sem("prd_ready")
        yT_ready = sem("yT_ready")
        xbo_ready = sem("xbo_ready")
        sum_ready = sem("sum_ready")
        stat_ready = sem("stat_ready")
        mv_ready = sem("mv_ready")
        veps_ready = sem("veps_ready")
        rstd_ready = sem("rstd_ready")
        norm_ready = sem("norm_ready")
        x1h_ready = sem("x1h_ready")
        x1l_ready = sem("x1l_ready")
        act_ready = sem("act_ready")
        gate_ready = sem("gate_ready")
        hi_ready = sem("hi_ready")
        lo_ready = sem("lo_ready")
        z_ready = sem("z_ready")
        wr_ready = sem("wr_ready")
        wdiff_ready = sem("wdiff_ready")
        wabs_ready = sem("wabs_ready")
        wflag_ready = sem("wflag_ready")
        stored = sem("stored")

        def full(eng, key):
            b, n, _ = bank[key]
            eng.wait_ge(bank_full[b], n + 1)
            return psum[:, b, :]

        def norm_no(which, c):
            order = [(0 if s[0] == "wo" else 1, s[1]) for s in steps if s[0] in ("wo", "ztr")]
            return order.index((which, c))

        def read(key):
            kind, i = key[0], key[1:]
            if kind == "spec":
                return spec_ready, 4
            if kind == "wtest":
                return wflag_ready, 1
            if kind == "qkv":
                return qkv_ready, i[0] * TPG + i[1] + 1
            if kind == "fwd":
                return prod_ready, 4 * (FB * i[0] + i[1]) + (3 if i[2] == "im" else 4)
            if kind == "inv":
                return k2_ready, i[0] * LB + i[1] + 1
            if kind == "head":
                return prd_ready, i[0] * H + i[1] + 1
            if kind in ("wo", "ztr"):
                return sum_ready, norm_no(int(kind == "ztr"), i[0]) + 1
            if kind == "up" and i[2] == 2:
                return gate_ready, gate_no(i[0], i[1]) + 1
            if kind in ("up", "hid"):
                return act_ready, place[i if kind == "hid" else (0,) + i[:2]] + 1
            return {"ytr": yT_ready, "x1tr": x1l_ready, "down": z_ready}[kind], i[0] + 1

        def gate_no(c, ob):
            return sum(b[0] == 0 for b in blocks[:place[(0, c, ob)]])

        def tiles(c):
            return tok[:, c * CT:(c + 1) * CT, 0, :]

        def reader_of(layer, c):
            return ("hid", layer + 1, c, KB - 1) if layer < 2 else ("down", c)

        block = ctx.enter_context(nc.Block())

        @block.sync
        def _(sp):
            sp.dma_start(kkT[:], a["kkT"]).then_inc(loaded["kk"], 16)
            sp.dma_start(kd[:], a["kd"]).then_inc(loaded["kk"], 16)
            sp.dma_start(mask[:], a["mask"]).then_inc(loaded["kk"], 16)
            sp.dma_start(dft[:], a["dft"]).then_inc(loaded["dft"], 16)
            half = TPG
            sp.dma_start(xT[:, 0:half, :], a["xT"][:, 0:half, :]).then_inc(loaded["xT0"], 16)
            sp.dma_start(idft[:], a["idft"]).then_inc(loaded["idft"], 16)
            sp.dma_start(xT[:, half:, :], a["xT"][:, half:, :]).then_inc(loaded["xT1"], 16)
            sp.dma_start(toep[:], a["toep"]).then_inc(loaded["toep"], 16)
            o = 0
            for name in ("w1T", "w2T", "h1T", "h2T", "w3T"):
                n = a[name].shape[1]
                sp.dma_start(w[:, o:o + n], a[name]).then_inc(loaded["w"], 16)
                o += n
            for g in range(G):
                full(sp, ("fwd", g, 1, "im"))
                for c in (2 * g, 2 * g + 1):
                    sp.dma_start(tiles(c), a["x"][c]).then_inc(loaded[f"x{g}"], 16)
            for c in range(CHUNKS):
                sp.wait_ge(norm_ready, CT * (norm_no(1, c) + 1))
                sp.dma_start(a["out"][c], tiles(c)).then_inc(stored, 16)
            sp.wait_ge(stored, 16 * CHUNKS)

        @block.gpsimd
        def _(pool):
            nc.gpsimd.memset(ident[:], 0.0).then_inc(const_ready, 1)
            nc.gpsimd.memset(ones[:], 1.0).then_inc(const_ready, 1)
            nc.gpsimd.memset(halves[:], -0.5).then_inc(const_ready, 1)
            pool.wait_ge(const_ready, 3)
            nc.gpsimd.affine_select(out=ident[:], in_=ident[:], compare_op=ALU.not_equal, fill=1.0, base=0,
                                    pattern=[[-1, P]], channel_multiplier=1).then_inc(const_ready, 1)
            made = [0]
            for s in steps:
                if s[0] == "fwd":
                    _, g, fb = s
                    pool.wait_ge(prod_ready, 4 * (FB * g + fb + 1))
                    if g:
                        full(pool, ("inv", g - 1, LB - 1))
                    nc.gpsimd.tensor_tensor(ys[:, fb, :], prod[:, fb, 0, :], prod[:, fb, 1, :], ALU.subtract)\
                        .then_inc(ys_ready, 1)
                    nc.gpsimd.tensor_tensor(ys[:, FB + fb, :], prod[:, fb, 2, :], prod[:, fb, 3, :], ALU.add)\
                        .then_inc(ys_ready, 1)
                    if fb == FB - 1:
                        pool.wait_ge(loaded[f"x{g}"], 16 * LB)
                        pool.wait_ge(loaded["small"], 16 * SMALL)
                        v = tok[:, g * TPG:(g + 1) * TPG, 0, :]
                        nc.gpsimd.tensor_tensor(v, v, bo[:].unsqueeze(1).broadcast_to([P, TPG, P]), ALU.add)\
                            .then_inc(xbo_ready, 1)
                elif s[0] == "weights":
                    for i in range(NW // SEG):
                        sl = slice(i * SEG, (i + 1) * SEG)
                        pool.wait_ge(wr_ready, i + 1)
                        if i:
                            pool.wait_ge(wabs_ready, i)
                        nc.gpsimd.tensor_tensor(wdiff[:], w[:, sl], wr[:, sl].bitcast(F32), ALU.subtract)\
                            .then_inc(wdiff_ready, 1)
                elif s[0] in ("wo", "ztr"):
                    which, c = int(s[0] == "ztr"), s[1]
                    n = norm_no(which, c)
                    pool.wait_ge(mv_ready, CT * (n + 1))
                    nc.gpsimd.tensor_scalar(rstd[:, which, c, 0, :], mv[:, which, c, :, 1], EPS, None, ALU.add)\
                        .then_inc(veps_ready, 1)
                    pool.wait_ge(veps_ready, n + 1)
                    nc.gpsimd.tensor_tensor(rstd[:, which, c, 1, :], rstd[:, which, c, 0, :], halves[:], ALU.pow)\
                        .then_inc(rstd_ready, 1)

        @block.scalar
        def _(act):
            act.dma_start(wqkv[:], a["wqkv"]).then_inc(loaded["wqkv"], 16)
            act.dma_start(bqkv[:], a["bqkv"].partition_broadcast(P)).then_inc(loaded["wqkv"], 16)
            for t, name in ((woT, "woT"), (scales, "scales"), (s3, "s3")):
                act.dma_start(t[:], a[name]).then_inc(loaded["small"], 16)
            act.dma_start(bo[:], a["bo"].partition_broadcast(P)).then_inc(loaded["small"], 16)
            act.dma_start(dcol[:], a["dd"].partition_broadcast(P)).then_inc(loaded["small"], 16)
            act.wait_ge(loaded["small"], 16 * SMALL)
            pending = []

            def high_part():
                if not pending:
                    return
                layer, c, ob = b = pending.pop()
                n = place[b]
                if layer == 0:
                    act.wait_ge(gate_ready, gate_no(c, ob) + 1)
                act.wait_ge(act_ready, n + 1)
                h = hidden_no[(layer, c)]
                if h >= 3:
                    full(act, reader_of(*layers[h - 3]))
                nc.scalar.activation(hidden[:, h % 3, 0, ob, :], ring[:, n % RING, :], ACT.Copy)\
                    .then_inc(hi_ready, 1)

            for s in steps:
                if s[0] == "inv":
                    _, g, lb = s
                    src = full(act, s)
                    ins = nc.scalar.activation(k2[:, g, lb * B:(lb + 1) * B, :],
                                               src.rearrange("p (b e) -> p b e", b=B), ACT.Copy)
                    ins.then_inc(k2_ready, 1)
                elif s[0] == "weights":
                    act.wait_ge(loaded["w"], 16 * 5)
                    for i in range(NW // SEG):
                        nc.scalar.activation(wr[:, i * SEG:(i + 1) * SEG], w[:, i * SEG:(i + 1) * SEG], ACT.Copy)\
                            .then_inc(wr_ready, 1)
                elif s[0] == "ytr":
                    c = s[1]
                    src = full(act, s)
                    if c >= LB:
                        full(act, ("wo", c - LB))
                    if c == 0:
                        for i in range(NW // SEG):
                            act.wait_ge(wdiff_ready, i + 1)
                            nc.scalar.activation(wdiff[:], wdiff[:], ACT.Abs, accum_out=wsum[:, i:i + 1])\
                                .then_inc(wabs_ready, 1)
                    ins = nc.scalar.activation(yT[:, c % LB, :], src, ACT.Copy)
                    ins.then_inc(yT_ready, 1)
                elif s[0] == "x1tr":
                    c = s[1]
                    src = full(act, s)
                    if c >= LB:
                        full(act, ("up", c - LB, KB - 1, 2))
                    nc.scalar.activation(x1T[:, 0, c % LB, :], src, ACT.Copy).then_inc(x1h_ready, 1)
                elif s[0] == "wtest":
                    src = full(act, s)
                    nc.scalar.activation(wflag[:, 1:], src[0:1, 0:NW // SEG], ACT.Copy, accum_out=wflag[:, 0:1])\
                        .then_inc(wflag_ready, 1)
                elif s[0] in ("up", "hid"):
                    if s[0] == "up":
                        _, c, ob = s
                        b, key, func, sc = (0, c, ob), s + (1,), ACT.Silu, scales[:, 0, ob:ob + 1]
                    else:
                        _, layer, c, ob = s
                        b, key, func, sc = (layer, c, ob), s, ACT.Gelu, scales[:, 1 + layer, ob:ob + 1]
                    n = place[b]
                    src = full(act, key)
                    if n >= RING:
                        act.wait_ge(lo_ready, n - RING + 1)
                    ins = nc.scalar.activation(ring[:, n % RING, :], src, func, scale=sc)
                    ins.then_inc(act_ready, 1)
                    high_part()
                    pending.append(b)
                elif s[0] == "down":
                    high_part()
                    c = s[1]
                    src = full(act, s)
                    if c:
                        full(act, ("ztr", c - 1))
                    ins = nc.scalar.activation(z[:], src, ACT.Copy, scale=s3[:, 0:1])
                    ins.then_inc(z_ready, 1)

        @block.vector
        def _(dve):
            v = nc.vector
            pending = []
            unnormed = []
            sums = [0]

            def low_part():
                if not pending:
                    return
                layer, c, ob = b = pending.pop()
                n = place[b]
                dve.wait_ge(hi_ready, n + 1)
                h = hidden_no[(layer, c)] % 3
                v.tensor_tensor(hidden[:, h, 1, ob, :], ring[:, n % RING, :], hidden[:, h, 0, ob, :].bitcast(F32),
                                ALU.subtract).then_inc(lo_ready, 1)

            def head_kv(g, h):
                n = g * H + h
                if n >= 3:
                    full(dve, ("head", (n - 3) // H, (n - 3) % H))
                ks = k2[:, g, :, h * NH:(h + 1) * NH].unsqueeze(3).broadcast_to([P, TPG, NH, NH])
                vs = tok[:, g * TPG:(g + 1) * TPG, 1, h * NH:(h + 1) * NH].unsqueeze(2)\
                    .broadcast_to([P, TPG, NH, NH])
                v.tensor_tensor(kv[:, n % 3], ks, vs, ALU.mult).then_inc(kv_ready, 1)

            def residual_and_stats(key, which, c):
                n = norm_no(which, c)
                src = full(dve, key)
                t = tiles(c)
                ins = v.tensor_tensor(t, src.rearrange("p (b e) -> p b e", b=CT), t, ALU.add)
                ins.then_inc(sum_ready, 1)
                dve.wait_ge(sum_ready, n + 1)
                for i in range(CT):
                    v.bn_stats(stats[:, which, c, i, :], t[:, i, :]).then_inc(stat_ready, 1)
                for i in range(CT):
                    dve.wait_ge(stat_ready, CT * n + i + 1)
                    v.bn_aggr(mv[:, which, c, i, :], stats[:, which, c, i, :]).then_inc(mv_ready, 1)
                unnormed.append((which, c))

            def normalise():
                while unnormed:
                    which, c = unnormed.pop(0)
                    n = norm_no(which, c)
                    dve.wait_ge(rstd_ready, n + 1)
                    for i in range(CT):
                        t = tok[:, c * CT + i, 0, :]
                        v.tensor_scalar(t, t, mv[:, which, c, i, 0:1], rstd[:, which, c, 1, i:i + 1],
                                        ALU.subtract, ALU.mult).then_inc(norm_ready, 1)

            dve.wait_ge(loaded["kk"], 16 * 3)
            v.tensor_tensor(kkT[0:1, 0, :], kkT[0:1, 0, :], kd[:], ALU.add).then_inc(kk_ready, 1)
            for s in steps:
                if s[0] == "spec":
                    src = full(dve, s)
                    re, im = src[:, 0:FB * P], src[:, FB * P:]
                    v.tensor_copy(spec_a[:], re.rearrange("p (f e) -> p f e", f=FB)).then_inc(spec_ready, 1)
                    v.tensor_scalar(spec_b[:, 0, :], im[:, 0:P], mask[:, 0:1], None, ALU.mult).then_inc(spec_ready, 1)
                    v.tensor_copy(spec_b[:, 1, :], im[:, P:]).then_inc(spec_ready, 1)
                    ins = v.tensor_scalar(spec_t[:], im[:, 0:P], mask[:, 1:2], None, ALU.mult)
                    ins.then_inc(spec_ready, 1)
                    dve.wait_ge(spec_ready, 4)
                    v.scalar_tensor_tensor(out=spec_c[:], in0=spec_a[:, 0, :], scalar=mask[:, 0:1], in1=spec_t[:],
                                           op0=ALU.mult, op1=ALU.add).then_inc(spec_ready, 1)
                elif s[0] == "qkv":
                    _, g, t = s
                    if (g, t) == (0, 0):
                        dve.wait_ge(loaded["wqkv"], 32)
                    src = full(dve, s)
                    ins = v.tensor_tensor(tok[:, g * TPG + t, :, :], src[:, 0:3 * P].rearrange("p (s e) -> p s e", s=3),
                                          bqkv[:].rearrange("p (s e) -> p s e", s=3), ALU.add)
                    ins.then_inc(qkv_ready, 1)
                elif s[0] == "fwd":
                    _, g, fb = s
                    xr, xi = full(dve, s + ("re",)), full(dve, s + ("im",))
                    if g == 0:
                        dve.wait_ge(spec_ready, 5)
                    else:
                        dve.wait_ge(ys_ready, 2 * (FB * (g - 1) + fb + 1))
                    sa, sb_ = spec_a[:, fb, :], spec_b[:, fb, :]
                    sc = spec_c[:] if fb == 0 else spec_a[:, 1, :]
                    for i, (x, coef) in enumerate(((xr, sa), (xi, sb_), (xi, sc), (xr, sb_))):
                        ins = v.tensor_tensor(prod[:, fb, i, :].rearrange("p (b e) -> p b e", b=B),
                                              x.rearrange("p (b e) -> p b e", b=B),
                                              coef.unsqueeze(1).broadcast_to([P, B, P]), ALU.mult)
                        ins.then_inc(prod_ready, 1)
                elif s[0] == "toeplitz":
                    dve.wait_ge(loaded["toep"], 16)
                    dve.wait_ge(loaded["small"], 16 * SMALL)
                    dve.wait_ge(const_ready, 4)
                    for h in range(H):
                        v.scalar_tensor_tensor(out=toep[:, h, 0:P], in0=ident[:], scalar=dcol[:, h:h + 1],
                                               in1=toep[:, h, 0:P], op0=ALU.mult, op1=ALU.add).then_inc(toep_ready, 1)
                elif s[0] == "kv0":
                    g = s[1]
                    dve.wait_ge(qkv_ready, TPG * (g + 1))
                    dve.wait_ge(k2_ready, LB * (g + 1))
                    head_kv(g, 0)
                    head_kv(g, 1)
                elif s[0] == "head":
                    _, g, h = s
                    src = full(dve, s)
                    if g and h == 0:
                        full(dve, ("ytr", LB * g - 1))
                    qs = tok[:, g * TPG:(g + 1) * TPG, 2, h * NH:(h + 1) * NH].unsqueeze(3)\
                        .broadcast_to([P, TPG, NH, NH])
                    ins = v.tensor_tensor(prd[:, :, :, h, :], src.rearrange("p (t m n) -> p t m n", t=TPG, m=NH), qs,
                                          ALU.mult)
                    ins.then_inc(prd_ready, 1)
                    if h + 2 < H:
                        head_kv(g, h + 2)
                elif s[0] == "wo":
                    if s[1] % LB == 0:
                        dve.wait_ge(xbo_ready, s[1] // LB + 1)
                    residual_and_stats(s, 0, s[1])
                elif s[0] == "x1tr":
                    c = s[1]
                    normalise()
                    src = full(dve, s)
                    dve.wait_ge(x1h_ready, c + 1)
                    ins = v.tensor_tensor(x1T[:, 1, c % LB, :], src, x1T[:, 0, c % LB, :].bitcast(F32), ALU.subtract)
                    ins.then_inc(x1l_ready, 1)
                elif s[0] == "up":
                    _, c, ob = s
                    n = place[(0, c, ob)]
                    src = full(dve, s + (2,))
                    dve.wait_ge(act_ready, n + 1)
                    r = ring[:, n % RING, :]
                    ins = v.scalar_tensor_tensor(out=r, in0=src, scalar=scales[:, 1, ob:ob + 1], in1=r,
                                                 op0=ALU.mult, op1=ALU.mult)
                    ins.then_inc(gate_ready, 1)
                    low_part()
                    pending.append((0, c, ob))
                elif s[0] == "hid":
                    low_part()
                    normalise()
                    pending.append(s[1:])
                elif s[0] == "down":
                    low_part()
                elif s[0] == "ztr":
                    residual_and_stats(s, 1, s[1])
                elif s[0] == "end":
                    normalise()

        @block.tensor
        def _(pe):
            def into(key):
                b, _, before = bank[key]
                if before:
                    pe.wait_ge(*read(before))
                return psum[:, b, :]

            def done(ins, key):
                ins.then_inc(bank_full[bank[key][0]], 1)

            def attention(s):
                if s[0] == "spec":
                    pe.wait_ge(kk_ready, 1)
                    pe.wait_ge(loaded["dft"], 16)
                    out = into(s)
                    for f in range(2 * FB):
                        for lb in range(LB):
                            ins = nc.tensor.matmul(out[:, f * P:(f + 1) * P], dft[:, lb, f * P:(f + 1) * P],
                                                   kkT[:, lb, :], start=(lb == 0), stop=(lb == LB - 1))
                    done(ins, s)
                elif s[0] == "qkv":
                    _, g, t = s
                    pe.wait_ge(loaded["wqkv"], 32)
                    pe.wait_ge(loaded[f"xT{g}"], 16)
                    out = into(s)
                    done(nc.tensor.matmul(out[:, 0:3 * P], xT[:, g * TPG + t, :], wqkv[:], start=True, stop=True), s)
                elif s[0] == "fwd":
                    _, g, fb = s
                    pe.wait_ge(qkv_ready, TPG * (g + 1))
                    for part, f in (("re", fb), ("im", FB + fb)):
                        out = into(s + (part,))
                        for lb in range(LB):
                            t = g * TPG + lb * B
                            ins = nc.tensor.matmul(out, dft[:, lb, f * P:(f + 1) * P], tok[:, t:t + B, 0, :],
                                                   start=(lb == 0), stop=(lb == LB - 1))
                        done(ins, s + (part,))
                elif s[0] == "inv":
                    _, g, lb = s
                    pe.wait_ge(loaded["idft"], 16)
                    pe.wait_ge(ys_ready, 2 * FB * (g + 1))
                    out = into(s)
                    for f in range(2 * FB):
                        ins = nc.tensor.matmul(out, idft[:, f, lb * P:(lb + 1) * P], ys[:, f, :],
                                               start=(f == 0), stop=(f == 2 * FB - 1))
                    done(ins, s)
                elif s[0] == "head":
                    _, g, h = s
                    n = g * H + h
                    pe.wait_ge(toep_ready, H)
                    pe.wait_ge(kv_ready, n + 1)
                    out = into(s)
                    half = B * NH * NH
                    x = kv[:, n % 3].rearrange("p t m n -> p (t m n)")
                    nc.tensor.matmul(out[:, 0:half], toep[:, h, 0:P], x[:, 0:half], start=True, stop=True)
                    nc.tensor.matmul(out[:, half:], toep[:, h, P:], x[:, 0:half], start=True, stop=False)
                    done(nc.tensor.matmul(out[:, half:], toep[:, h, 0:P], x[:, half:], start=False, stop=True), s)
                elif s[0] == "ytr":
                    c = s[1]
                    pe.wait_ge(prd_ready, H * (c // LB + 1))
                    pe.wait_ge(const_ready, 4)
                    out = into(s)
                    for b in range(B):
                        for m in range(NH):
                            ins = nc.tensor.matmul(out[:, b * P:(b + 1) * P],
                                                   prd[:, (c % LB) * B + b, m].rearrange("p h n -> p (h n)"),
                                                   ident[:], start=(m == 0), stop=(m == NH - 1), is_transpose=True)
                    done(ins, s)
                elif s[0] == "wo":
                    c = s[1]
                    pe.wait_ge(yT_ready, c + 1)
                    pe.wait_ge(loaded["small"], 16 * SMALL)
                    out = into(s)
                    for b in range(B):
                        ins = nc.tensor.matmul(out[:, b * P:(b + 1) * P], yT[:, c % LB, b * P:(b + 1) * P], woT[:],
                                               start=True, stop=True)
                    done(ins, s)
                elif s[0] == "wtest":
                    pe.wait_ge(wabs_ready, NW // SEG)
                    out = into(s)
                    done(nc.tensor.matmul(out[0:1, 0:NW // SEG], ones[:], wsum[:], start=True, stop=True), s)
                elif s[0] == "x1tr":
                    c = s[1]
                    pe.wait_ge(norm_ready, CT * (norm_no(0, c) + 1))
                    out = into(s)
                    for b in range(CT):
                        ins = nc.tensor.transpose(out[:, b * P:(b + 1) * P], tok[:, c * CT + b, 0, :], ident[:])
                    done(ins, s)

            def products(out, pairs, exact):
                todo = [(p, part) for p in pairs for part in (0, 1)]
                for i, ((which, k, ob, x), part) in enumerate(todo):
                    wt, xt = w_of(wr if exact else w, which, k, ob), x(part)
                    if not exact:
                        xt = xt.bitcast(F32)
                    ins = nc.tensor.matmul(out, wt, xt, start=(i == 0), stop=(i == len(todo) - 1))
                return ins

            def feed_forward(s, exact):
                if s[0] == "up":
                    _, c, ob = s
                    pe.wait_ge(x1l_ready, c + 1)
                    for which in (0, 1):
                        key = s + (which + 1,)
                        out = into(key)
                        done(products(out, [(which, 0, ob, lambda p: x1T[:, p, c % LB, :])], exact), key)
                elif s[0] in ("hid", "down"):
                    layer, c = (s[1], s[2]) if s[0] == "hid" else (3, s[1])
                    ob = s[3] if s[0] == "hid" else 0
                    n = hidden_no[(layer - 1, c)] % 3
                    pe.wait_ge(lo_ready, place[(layer - 1, c, KB - 1)] + 1)
                    out = into(s)
                    pairs = [(layer + 1, k, ob, lambda p, k=k: hidden[:, n, p, k, :]) for k in range(KB)]
                    done(products(out, pairs, exact), s)
                elif s[0] == "ztr":
                    c = s[1]
                    pe.wait_ge(z_ready, c + 1)
                    out = into(s)
                    for b in range(CT):
                        ins = nc.tensor.transpose(out[:, b * P:(b + 1) * P], z[:, b * P:(b + 1) * P], ident[:])
                    done(ins, s)

            start = next(i for i, s in enumerate(steps) if s[0] == "up")
            for s in steps[:start]:
                attention(s)
            pe.wait_ge(wflag_ready, 1)
            flag = pe.value_load(wflag[:, 0:1].bitcast(I32))
            with pe.If(flag == 0):
                for s in steps[start:]:
                    attention(s)
                    feed_forward(s, True)
            with pe.Else():
                for s in steps[start:]:
                    attention(s)
                    feed_forward(s, False)


SMALL = 5


def constants():
    import numpy as np

    n = 2 * L
    pos, f = np.arange(L), np.arange(FB * P)
    ang = 2 * np.pi * np.outer(pos, f) / n
    cos, sin = np.cos(ang), np.sin(ang)
    nyquist = np.cos(np.pi * pos)
    im = -sin
    im[:, 0] = nyquist
    fwd = np.concatenate([cos, im], axis=1)
    back_re = 2 * cos.T / n
    back_re[0] /= 2
    back_im = -2 * sin.T / n
    back_im[0] = nyquist / n
    back = np.concatenate([back_re, back_im])
    mask = np.zeros((P, 2))
    mask[1:, 0] = 1
    mask[0, 1] = 1
    f32 = lambda x: np.ascontiguousarray(x, dtype=np.float32)
    return {
        "dft": f32(fwd.reshape(LB, P, -1).transpose(1, 0, 2)),
        "idft": f32(back.reshape(2 * FB, P, L).transpose(1, 0, 2)),
        "mask": f32(mask),
    }


def kernel(**inputs):
    import numpy as np
    import concourse.bacc as bacc
    from concourse.bass_utils import run_bass_kernel_spmd

    i = {k.replace("L0_", "").replace("attn_", ""): np.asarray(v) for k, v in inputs.items()}
    x = i["u"]
    tiled = x.reshape(G, B, LB, P, D).transpose(0, 2, 3, 1, 4)

    def cols(name):
        wt = i[name].T
        return wt.reshape(-1, P, wt.shape[1]).transpose(1, 0, 2).reshape(P, -1)

    padded = np.concatenate([np.zeros((H, P - 1), np.float32), i["ssm_kernel"]], axis=1)

    arrays = constants() | {
        "xT": x.reshape(G, B, LB, P, D).transpose(4, 0, 2, 1, 3).reshape(D, TILES, P),
        "x": tiled.reshape(CHUNKS, P, CT, D),
        "wqkv": np.concatenate([i["Wk"].T, i["Wv"].T, i["Wq"].T], axis=1),
        "bqkv": np.concatenate([i["bk"], i["bv"], i["bq"]]),
        "kkT": i["ssm_k_kernel"].T.reshape(LB, P, D).transpose(1, 0, 2),
        "kd": i["ssm_k_D"][None, :],
        "toep": padded[:, P - 1 + np.arange(L)[None] - np.arange(P)[:, None]].transpose(1, 0, 2),
        "dd": i["D"],
        "woT": i["Wo"].T.reshape(NH, H, D).transpose(1, 0, 2).reshape(D, D),
        "bo": i["bo"],
        "w1T": cols("ffn_w1_w"), "w2T": cols("ffn_w2_w"), "h1T": cols("ffn_h1_w"), "h2T": cols("ffn_h2_w"),
        "w3T": cols("ffn_w3_w"),
        "scales": np.stack([i[f"ffn_{n}_s"].reshape(KB, P).T for n in ("w1", "w2", "h1", "h2")], axis=1),
        "s3": i["ffn_w3_s"][:, None],
    }
    arrays = {k: np.ascontiguousarray(v) for k, v in arrays.items()}
    nc = bacc.Bacc("TRN2", target_bir_lowering=False, num_devices=1)
    aps = {k: nc.dram_tensor(f"in_{k}", v.shape, F32, kind="ExternalInput").ap() for k, v in arrays.items()}
    aps["out"] = nc.dram_tensor("out_x", (CHUNKS, P, CT, D), F32, kind="ExternalOutput").ap()
    build(nc, aps)
    r = run_bass_kernel_spmd(nc, [{f"in_{k}": v for k, v in arrays.items()}], core_ids=[0])
    out = r.results[0]["out_x"].reshape(G, LB, P, B, D)
    return np.ascontiguousarray(out.transpose(0, 3, 1, 2, 4)).reshape(BATCH, L, D)
```

```python
from contextlib import ExitStack

import concourse.bass as bass
from concourse import mybir

F32 = mybir.dt.float32
F32R = mybir.dt.float32r
BF16 = mybir.dt.bfloat16
I32 = mybir.dt.int32
ALU = mybir.AluOpType
ACT = mybir.ActivationFunctionType
AX = mybir.AxisListType

P = 128
BATCH, L, D = 8, 256, 128
NH = 8
H = D // NH
G, B, LB = 2, 4, L // P
TPG = LB * B
TILES = G * TPG
CHUNKS, CT = G * LB, B
CW = CT * P
HID = 512
KB = HID // P
EPS = 1e-5
SEG = 1408
FB = 2


def step_order():
    def heads(g, lo, hi):
        return [("head", g, h) for h in range(lo, hi)]

    first = [("qkv", 0, t) for t in range(6)] + [("kk",), ("qkv", 0, 6), ("qkv", 0, 7), ("ksplit", 0), ("spec",)]
    first += [("fwd", 0, 0), ("fwd", 0, 1)] + [("qkv", 1, t) for t in range(2)] + [("ysplit", 0, 0)]
    first += [("qkv", 1, t) for t in range(2, 5)] + [("ysplit", 0, 1)] + [("qkv", 1, t) for t in range(5, TPG)]
    first += [("ksplit", 1), ("inv", 0, 0), ("inv", 0, 1), ("toeplitz",), ("kv0", 0), ("fwd", 1, 0)]
    first += heads(0, 0, 1) + [("fwd", 1, 1), ("ysplit", 1, 0)] + heads(0, 1, 3) + [("ysplit", 1, 1), ("xbo", 0)]
    first += heads(0, 3, 5) + [("inv", 1, 0)] + heads(0, 5, 7) + [("inv", 1, 1)] + heads(0, 7, 8)
    for i in range(4):
        first += [("weights", i)] + heads(0, 8 + i, 9 + i)
    first += heads(0, 12, 14) + [("xbo", 1)] + heads(0, 14, 16)
    first += [("sumend",), ("kv0", 1), ("head", 1, 0), ("head", 1, 1), ("ytr", 0), ("head", 1, 2), ("ytr", 1), ("wtest",)]
    first += [("head", 1, 3), ("wo", 0), ("head", 1, 4), ("wo", 1)] + heads(1, 5, 8) + [("x1tr", 0)]
    first += heads(1, 8, 9) + [("x1tr", 1)]

    def ffn(g):
        a, b = 2 * g, 2 * g + 1
        out = [("up", c, ob) for c in (a, b) for ob in range(KB)]
        out += [("hid", layer, c, ob) for layer in (1, 2) for c in (a, b) for ob in range(KB)]
        return out + [("down", a), ("down", b), ("ztr", a), ("ztr", b)]

    rest = heads(1, 9, H)
    rest += [("sumend",), ("ytr", 2), ("ytr", 3), ("wo", 2), ("wo", 3), ("gap",), ("gap",), ("x1tr", 2), ("x1tr", 3)]
    merged = []
    for i, item in enumerate(ffn(0)):
        merged.append(item)
        if rest:
            merged.append(rest.pop(0))
    return first + merged + rest + ffn(1) + [("end",)]


def banks_of(steps):
    at, used, last, turn = {}, [0] * 8, [None] * 8, {}

    def take(key, pool):
        n = turn.get(pool, 0)
        turn[pool] = n + 1
        bank = pool[n % len(pool)]
        at[key] = (bank, used[bank], last[bank])
        used[bank] += 1
        last[bank] = key

    front, side, every = (0, 1, 2, 3), (4, 5, 6, 7), tuple(range(8))
    heads_done = False
    for s in steps:
        late = every if heads_done else side
        if s[0] == "spec" or s[0] in ("qkv", "inv"):
            take(s, side)
        elif s[0] == "fwd":
            take(s + ("re",), front)
            take(s + ("im",), front)
        elif s[0] == "head":
            take(s, front)
            heads_done = s == ("head", 1, H - 1)
        elif s[0] == "up":
            take(s + (1,), late)
            take(s + (2,), late)
        elif s[0] == "wtest":
            take(s, side)
        elif s[0] in ("ytr", "wo", "x1tr", "hid", "down", "ztr"):
            take(s, late)
    return at


def build(nc, a):
    steps = step_order()
    bank = banks_of(steps)
    blocks = [(0,) + s[1:] if s[0] == "up" else s[1:] for s in steps if s[0] in ("up", "hid")]
    place = {b: n for n, b in enumerate(blocks)}
    layers = sorted({b[:2] for b in blocks}, key=lambda lc: place[lc + (0,)])
    hidden_no = {lc: n for n, lc in enumerate(layers)}
    RING = 4
    KVR = 4

    with ExitStack() as ctx:
        def sb(name, shape, dt=F32):
            return ctx.enter_context(nc.sbuf_tensor(name, shape, dt))

        def sem(name):
            return ctx.enter_context(nc.semaphore(name))

        tok = sb("tok", [P, TILES, 3, P])
        k2 = sb("k2", [P, G, TPG, P])
        toep = sb("toep", [P, H, L])
        kv = sb("kv", [P, KVR, TPG, NH, NH])
        qy = sb("qy", [P, 2, TPG, NH, NH])
        y = sb("y", [P, TPG, H, NH])
        yT = sb("yT", [P, LB, CW])
        x1T = sb("x1T", [P, 2, LB, CW], F32R)
        NW = (2 + 2 * KB) * HID + KB * P
        z = sb("z", [P, CW])
        ident = sb("ident", [P, P])
        wqkv = sb("wqkv", [P, 3 * P])
        bqkv = sb("bqkv", [P, 3 * P])
        woT = sb("woT", [P, P])
        bo = sb("bo", [P, P])
        dcol = sb("dcol", [P, H])
        kd = sb("kd", [1, P])
        mask = sb("mask", [P, 2])
        scales = sb("scales", [P, 4, KB])
        s3 = sb("s3", [P, 1])
        w = sb("w", [P, NW])
        wbits = sb("wbits", [P, 2, SEG], I32)
        ones = sb("ones", [P, 1])
        halves = sb("halves", [P, CT])
        stats = sb("stats", [P, 2, CHUNKS, CT, nc.vector.BN_STATS_DIM])
        mv = sb("mv", [P, 2, CHUNKS, CT, nc.vector.BN_AGGR_DIM])
        rstd = sb("rstd", [P, 2, CHUNKS, 2, CT])
        wsum = sb("wsum", [P, NW // SEG])
        wflag = sb("wflag", [1, NW // SEG + 1])

        early = ctx.enter_context(ExitStack())

        def esb(name, shape, dt=F32):
            return early.enter_context(nc.sbuf_tensor(name, shape, dt))

        xT = esb("xT", [P, TILES, P])
        dft = esb("dft", [P, LB, 4 * P])
        idft = esb("idft", [P, 2 * FB, L])
        kkT = esb("kkT", [P, LB, P])
        spec_a, spec_b = esb("spec_a", [P, FB, P]), esb("spec_b", [P, FB, P])
        spec_c, spec_t = esb("spec_c", [P, P]), esb("spec_t", [P, P])
        dftr = esb("dftr", [P, 2, LB, 4 * P], F32R)
        idftr = esb("idftr", [P, 2, 2 * FB, L], F32R)
        kr = esb("kr", [P, 2, TPG, P], F32R)
        ysr = esb("ysr", [P, 2, 2 * FB, CW], F32R)
        prod = esb("prod", [P, FB, 4, CW])
        ys = esb("ys", [P, 2 * FB, CW])
        early.close()
        hidden = sb("hidden", [P, 3, 2, KB, CW], F32R)
        ring = sb("ring", [P, RING, CW])
        wr = sb("wr", [P, NW], F32R)

        psum = ctx.enter_context(nc.psum_tensor("psum", [P, 8, 512], F32))

        def w_of(t, which, k, ob):
            if which < 2:
                lo = which * HID + ob * P
            elif which < 4:
                lo = (2 + (which - 2) * KB + k) * HID + ob * P
            else:
                lo = (2 + 2 * KB) * HID + k * P
            return t[:, lo:lo + P]

        loads = ["kk", "dft", "wqkv", "bqkv", "xT0", "xT1", "xT2", "xT3", "xT4", "idft", "toep", "small", "w", "x0", "x1"]
        loaded = {n: sem(f"loaded_{n}") for n in loads}
        bank_full = [sem(f"bank_full{i}") for i in range(8)]
        const_ready = sem("const_ready")
        kk_ready = sem("kk_ready")
        spec_ready = sem("spec_ready")
        qkv_ready = sem("qkv_ready")
        prod_ready = sem("prod_ready")
        ys_ready = sem("ys_ready")
        k2_ready = sem("k2_ready")
        toep_ready = sem("toep_ready")
        kv_ready = sem("kv_ready")
        qy_ready = sem("qy_ready")
        y_ready = sem("y_ready")
        split_ready = sem("split_ready")
        dftr_ready = sem("dftr_ready")
        idftr_ready = sem("idftr_ready")
        kh_ready = sem("kh_ready")
        kr0_ready = sem("kr0_ready")
        kr1_ready = sem("kr1_ready")
        yh_ready = sem("yh_ready")
        ysr_ready = sem("ysr_ready")
        yT_ready = sem("yT_ready")
        xbo_ready = sem("xbo_ready")
        sum_ready = sem("sum_ready")
        stat_ready = sem("stat_ready")
        mv_ready = sem("mv_ready")
        veps_ready = sem("veps_ready")
        rstd_ready = sem("rstd_ready")
        norm_ready = sem("norm_ready")
        x1h_ready = sem("x1h_ready")
        x1l_ready = sem("x1l_ready")
        act_ready = sem("act_ready")
        gate_ready = sem("gate_ready")
        hi_ready = sem("hi_ready")
        lo_ready = sem("lo_ready")
        lop_ready = sem("lop_ready")
        z_ready = sem("z_ready")
        wr_ready = sem("wr_ready")
        wbits_ready = sem("wbits_ready")
        wsum_ready = sem("wsum_ready")
        wflag_ready = sem("wflag_ready")
        stored = sem("stored")

        def full(eng, key):
            b, n, _ = bank[key]
            eng.wait_ge(bank_full[b], n + 1)
            return psum[:, b, :]

        def norm_no(which, c):
            order = [(0 if s[0] == "wo" else 1, s[1]) for s in steps if s[0] in ("wo", "ztr")]
            return order.index((which, c))

        def read(key):
            kind, i = key[0], key[1:]
            if kind == "spec":
                return spec_ready, 4
            if kind == "wtest":
                return wflag_ready, 1
            if kind == "qkv":
                return qkv_ready, i[0] * TPG + i[1] + 1
            if kind == "fwd":
                return prod_ready, 4 * (FB * i[0] + i[1]) + (3 if i[2] == "im" else 4)
            if kind == "inv":
                return k2_ready, i[0] * LB + i[1] + 1
            if kind == "head":
                return qy_ready, i[0] * H + i[1] + 1
            if kind in ("wo", "ztr"):
                return sum_ready, norm_no(int(kind == "ztr"), i[0]) + 1
            if kind == "up" and i[2] == 2:
                return gate_ready, gate_no(i[0], i[1]) + 1
            if kind in ("up", "hid"):
                return act_ready, place[i if kind == "hid" else (0,) + i[:2]] + 1
            return {"ytr": yT_ready, "x1tr": x1l_ready, "down": z_ready}[kind], i[0] + 1

        def pool_makes(b):
            return b[0] == 0 and b[2] % 2 == 1

        def low_parts(eng, n):
            by_pool = sum(map(pool_makes, blocks[:n + 1]))
            if n + 1 > by_pool:
                eng.wait_ge(lo_ready, n + 1 - by_pool)
            if by_pool:
                eng.wait_ge(lop_ready, by_pool)

        def gate_no(c, ob):
            return sum(b[0] == 0 for b in blocks[:place[(0, c, ob)]])

        def tiles(c):
            return tok[:, c * CT:(c + 1) * CT, 0, :]

        def reader_of(layer, c):
            return ("hid", layer + 1, c, KB - 1) if layer < 2 else ("down", c)

        block = ctx.enter_context(nc.Block())

        @block.sync
        def _(sp):
            sp.dma_start(wqkv[:], a["wqkv"]).then_inc(loaded["wqkv"], 16)
            for i, (lo, hi) in enumerate(XT_PIECES):
                sp.dma_start(xT[:, lo:hi, :], a["xT"][:, lo:hi, :]).then_inc(loaded[f"xT{i}"], 16)
                if i == 1:
                    sp.dma_start(dft[:], a["dft"]).then_inc(loaded["dft"], 16)
                if i == 3:
                    sp.dma_start(idft[:], a["idft"]).then_inc(loaded["idft"], 16)
            sp.dma_start(toep[:], a["toep"]).then_inc(loaded["toep"], 16)
            o = 0
            for name in ("w1T", "w2T", "h1T", "h2T", "w3T"):
                n = a[name].shape[1]
                sp.dma_start(w[:, o:o + n], a[name]).then_inc(loaded["w"], 16)
                o += n
            for g in range(G):
                full(sp, ("fwd", g, 1, "im"))
                for c in (2 * g, 2 * g + 1):
                    sp.dma_start(tiles(c), a["x"][c]).then_inc(loaded[f"x{g}"], 16)
            for c in range(CHUNKS):
                sp.wait_ge(norm_ready, CT * (norm_no(1, c) + 1))
                sp.dma_start(a["out"][c], tiles(c)).then_inc(stored, 16)
            sp.wait_ge(stored, 16 * CHUNKS)

        @block.gpsimd
        def _(pool):
            nc.gpsimd.memset(ident[:], 0.0).then_inc(const_ready, 1)
            nc.gpsimd.memset(ones[:], 1.0).then_inc(const_ready, 1)
            nc.gpsimd.memset(halves[:], -0.5).then_inc(const_ready, 1)
            pool.wait_ge(const_ready, 3)
            nc.gpsimd.affine_select(out=ident[:], in_=ident[:], compare_op=ALU.not_equal, fill=1.0, base=0,
                                    pattern=[[-1, P]], channel_multiplier=1).then_inc(const_ready, 1)
            pool.wait_ge(loaded["small"], 16 * SMALL)

            def head_kv(g, h):
                n = g * H + h
                if n >= KVR:
                    full(pool, ("head", (n - KVR) // H, (n - KVR) % H))
                ks = k2[:, g, :, h * NH:(h + 1) * NH].unsqueeze(2).broadcast_to([P, TPG, NH, NH])
                vs = tok[:, g * TPG:(g + 1) * TPG, 1, h * NH:(h + 1) * NH].unsqueeze(3)\
                    .broadcast_to([P, TPG, NH, NH])
                nc.gpsimd.tensor_tensor(kv[:, n % KVR], vs, ks, ALU.mult).then_inc(kv_ready, 1)

            for s in steps:
                if s == ("fwd", 0, 0):
                    pool.wait_ge(split_ready, 2)
                    nc.gpsimd.tensor_tensor(idftr[:, 1], idft[:], idftr[:, 0].bitcast(F32), ALU.subtract)\
                        .then_inc(idftr_ready, 1)
                if s[0] == "fwd":
                    _, g, fb = s
                    pool.wait_ge(prod_ready, 4 * (FB * g + fb + 1))
                    if g:
                        pool.wait_ge(ysr_ready, 2 * (FB * (g - 1) + fb + 1))
                    nc.gpsimd.tensor_tensor(ys[:, fb, :], prod[:, fb, 0, :], prod[:, fb, 1, :], ALU.subtract)\
                        .then_inc(ys_ready, 1)
                    nc.gpsimd.tensor_tensor(ys[:, FB + fb, :], prod[:, fb, 2, :], prod[:, fb, 3, :], ALU.add)\
                        .then_inc(ys_ready, 1)
                elif s == ("ksplit", 1):
                    for lb in range(LB):
                        t = TPG + lb * B
                        pool.wait_ge(kh_ready, LB + lb + 1)
                        nc.gpsimd.tensor_tensor(kr[:, 1, lb * B:(lb + 1) * B, :], tok[:, t:t + B, 0, :],
                                                kr[:, 0, lb * B:(lb + 1) * B, :].bitcast(F32), ALU.subtract)\
                            .then_inc(kr1_ready, 1)
                elif s[0] == "xbo":
                    g = s[1]
                    pool.wait_ge(loaded[f"x{g}"], 16 * LB)
                    v = tok[:, g * TPG:(g + 1) * TPG, 0, :]
                    nc.gpsimd.tensor_tensor(v, v, bo[:].unsqueeze(1).broadcast_to([P, TPG, P]), ALU.add)\
                        .then_inc(xbo_ready, 1)
                elif s[0] == "kv0":
                    g = s[1]
                    pool.wait_ge(qkv_ready, TPG * (g + 1))
                    pool.wait_ge(k2_ready, LB * (g + 1))
                    for h in range(KVR - 1):
                        head_kv(g, h)
                elif s[0] == "head" and s[2] + KVR - 1 < H:
                    head_kv(s[1], s[2] + KVR - 1)
                elif s[0] == "up" and pool_makes((0,) + s[1:]):
                    _, c, ob = s
                    n = place[(0, c, ob)]
                    pool.wait_ge(hi_ready, n + 1)
                    h = hidden_no[(0, c)] % 3
                    nc.gpsimd.tensor_tensor(hidden[:, h, 1, ob, :], ring[:, n % RING, :],
                                            hidden[:, h, 0, ob, :].bitcast(F32), ALU.subtract).then_inc(lop_ready, 1)
                elif s[0] in ("wo", "ztr"):
                    which, c = int(s[0] == "ztr"), s[1]
                    n = norm_no(which, c)
                    pool.wait_ge(mv_ready, CT * (n + 1))
                    nc.gpsimd.tensor_scalar(rstd[:, which, c, 0, :], mv[:, which, c, :, 1], EPS, None, ALU.add)\
                        .then_inc(veps_ready, 1)
                    pool.wait_ge(veps_ready, n + 1)
                    nc.gpsimd.tensor_tensor(rstd[:, which, c, 1, :], rstd[:, which, c, 0, :], halves[:], ALU.pow)\
                        .then_inc(rstd_ready, 1)

        @block.scalar
        def _(act):
            act.dma_start(bqkv[:], a["bqkv"].partition_broadcast(P)).then_inc(loaded["bqkv"], 16)
            act.dma_start(kkT[:], a["kkT"]).then_inc(loaded["kk"], 16)
            act.dma_start(kd[:], a["kd"]).then_inc(loaded["kk"], 16)
            act.dma_start(mask[:], a["mask"]).then_inc(loaded["kk"], 16)
            for t, name in ((woT, "woT"), (scales, "scales"), (s3, "s3")):
                act.dma_start(t[:], a[name]).then_inc(loaded["small"], 16)
            act.dma_start(bo[:], a["bo"].partition_broadcast(P)).then_inc(loaded["small"], 16)
            act.dma_start(dcol[:], a["dd"].partition_broadcast(P)).then_inc(loaded["small"], 16)
            pending = []

            def high_part():
                if not pending:
                    return
                layer, c, ob = b = pending.pop()
                n = place[b]
                if layer == 0:
                    act.wait_ge(gate_ready, gate_no(c, ob) + 1)
                act.wait_ge(act_ready, n + 1)
                h = hidden_no[(layer, c)]
                if h >= 3:
                    full(act, reader_of(*layers[h - 3]))
                nc.scalar.activation(hidden[:, h % 3, 0, ob, :], ring[:, n % RING, :], ACT.Copy)\
                    .then_inc(hi_ready, 1)

            for s in steps:
                if s[0] == "inv":
                    _, g, lb = s
                    src = full(act, s)
                    ins = nc.scalar.activation(k2[:, g, lb * B:(lb + 1) * B, :],
                                               src.rearrange("p (b e) -> p b e", b=B), ACT.Copy)
                    ins.then_inc(k2_ready, 1)
                elif s[0] == "kk":
                    act.wait_ge(loaded["dft"], 16)
                    nc.scalar.activation(dftr[:, 0], dft[:], ACT.Copy).then_inc(split_ready, 1)
                elif s[0] == "spec":
                    act.wait_ge(loaded["idft"], 16)
                    nc.scalar.activation(idftr[:, 0], idft[:], ACT.Copy).then_inc(split_ready, 1)
                elif s[0] == "ksplit":
                    g = s[1]
                    for lb in range(LB):
                        t = g * TPG + lb * B
                        act.wait_ge(qkv_ready, t + B)
                        if g:
                            full(act, ("fwd", g - 1, FB - 1, "im"))
                        nc.scalar.activation(kr[:, 0, lb * B:(lb + 1) * B, :], tok[:, t:t + B, 0, :], ACT.Copy)\
                            .then_inc(kh_ready, 1)
                elif s[0] == "ysplit":
                    _, g, fb = s
                    for i, f in enumerate((fb, FB + fb)):
                        act.wait_ge(ys_ready, 2 * (FB * g + fb) + i + 1)
                        if g:
                            full(act, ("inv", g - 1, LB - 1))
                        nc.scalar.activation(ysr[:, 0, f, :], ys[:, f, :], ACT.Copy).then_inc(yh_ready, 1)
                elif s[0] == "weights":
                    i = s[1]
                    act.wait_ge(loaded["w"], 16 * 5)
                    nc.scalar.activation(wr[:, i * SEG:(i + 1) * SEG], w[:, i * SEG:(i + 1) * SEG], ACT.Copy)\
                        .then_inc(wr_ready, 1)
                    act.wait_ge(wbits_ready, i + 1)
                    nc.scalar.activation(wbits[:, i % 2], wbits[:, i % 2], ACT.Copy, accum_out=wsum[:, i:i + 1])\
                        .then_inc(wsum_ready, 1)
                elif s[0] == "ytr":
                    c = s[1]
                    src = full(act, s)
                    if c >= LB:
                        full(act, ("wo", c - LB))
                    ins = nc.scalar.activation(yT[:, c % LB, :], src, ACT.Copy)
                    ins.then_inc(yT_ready, 1)
                elif s[0] == "x1tr":
                    c = s[1]
                    src = full(act, s)
                    if c >= LB:
                        full(act, ("up", c - LB, KB - 1, 2))
                    nc.scalar.activation(x1T[:, 0, c % LB, :], src, ACT.Copy).then_inc(x1h_ready, 1)
                elif s[0] == "wtest":
                    src = full(act, s)
                    nc.scalar.activation(wflag[:, 1:], src[0:1, 0:NW // SEG], ACT.Copy, accum_out=wflag[:, 0:1])\
                        .then_inc(wflag_ready, 1)
                elif s[0] in ("up", "hid"):
                    if s[0] == "up":
                        _, c, ob = s
                        b, key, func, sc = (0, c, ob), s + (1,), ACT.Silu, scales[:, 0, ob:ob + 1]
                    else:
                        _, layer, c, ob = s
                        b, key, func, sc = (layer, c, ob), s, ACT.Gelu, scales[:, 1 + layer, ob:ob + 1]
                    n = place[b]
                    if n == 0:
                        act.wait_ge(loaded["small"], 16 * SMALL)
                    src = full(act, key)
                    if n >= RING:
                        low_parts(act, n - RING)
                    ins = nc.scalar.activation(ring[:, n % RING, :], src, func, scale=sc)
                    ins.then_inc(act_ready, 1)
                    high_part()
                    pending.append(b)
                elif s[0] == "down":
                    high_part()
                    c = s[1]
                    src = full(act, s)
                    if c:
                        full(act, ("ztr", c - 1))
                    ins = nc.scalar.activation(z[:], src, ACT.Copy, scale=s3[:, 0:1])
                    ins.then_inc(z_ready, 1)

        @block.vector
        def _(dve):
            v = nc.vector
            pending = []
            unnormed, unsummed = [], []

            def low_part():
                if not pending:
                    return
                layer, c, ob = b = pending.pop()
                if pool_makes(b):
                    return
                n = place[b]
                dve.wait_ge(hi_ready, n + 1)
                h = hidden_no[(layer, c)] % 3
                v.tensor_tensor(hidden[:, h, 1, ob, :], ring[:, n % RING, :], hidden[:, h, 0, ob, :].bitcast(F32),
                                ALU.subtract).then_inc(lo_ready, 1)

            def head_sum():
                if not unsummed:
                    return
                g, h = unsummed.pop()
                n = g * H + h
                dve.wait_ge(qy_ready, n + 1)
                if g and h == 0:
                    full(dve, ("ytr", LB * g - 1))
                v.tensor_reduce(y[:, :, h, :], qy[:, n % 2], AX.X, ALU.add).then_inc(y_ready, 1)

            def residual_and_stats(key, which, c):
                n = norm_no(which, c)
                src = full(dve, key)
                t = tiles(c)
                ins = v.tensor_tensor(t, src.rearrange("p (b e) -> p b e", b=CT), t, ALU.add)
                ins.then_inc(sum_ready, 1)
                dve.wait_ge(sum_ready, n + 1)
                for i in range(CT):
                    v.bn_stats(stats[:, which, c, i, :], t[:, i, :]).then_inc(stat_ready, 1)
                for i in range(CT):
                    dve.wait_ge(stat_ready, CT * n + i + 1)
                    v.bn_aggr(mv[:, which, c, i, :], stats[:, which, c, i, :]).then_inc(mv_ready, 1)
                unnormed.append((which, c))

            def normalise():
                while unnormed:
                    which, c = unnormed.pop(0)
                    n = norm_no(which, c)
                    dve.wait_ge(rstd_ready, n + 1)
                    for i in range(CT):
                        t = tok[:, c * CT + i, 0, :]
                        v.tensor_scalar(t, t, mv[:, which, c, i, 0:1], rstd[:, which, c, 1, i:i + 1],
                                        ALU.subtract, ALU.mult).then_inc(norm_ready, 1)

            for s in steps:
                if s[0] == "kk":
                    dve.wait_ge(loaded["kk"], 16 * 3)
                    v.tensor_tensor(kkT[0:1, 0, :], kkT[0:1, 0, :], kd[:], ALU.add).then_inc(kk_ready, 1)
                    dve.wait_ge(split_ready, 1)
                    v.tensor_tensor(dftr[:, 1], dft[:], dftr[:, 0].bitcast(F32), ALU.subtract).then_inc(dftr_ready, 1)
                elif s == ("ksplit", 0):
                    for lb in range(LB):
                        t = lb * B
                        dve.wait_ge(kh_ready, lb + 1)
                        v.tensor_tensor(kr[:, 1, lb * B:(lb + 1) * B, :], tok[:, t:t + B, 0, :],
                                        kr[:, 0, lb * B:(lb + 1) * B, :].bitcast(F32), ALU.subtract)\
                            .then_inc(kr0_ready, 1)
                elif s[0] == "ysplit":
                    _, g, fb = s
                    for i, f in enumerate((fb, FB + fb)):
                        dve.wait_ge(yh_ready, 2 * (FB * g + fb) + i + 1)
                        v.tensor_tensor(ysr[:, 1, f, :], ys[:, f, :], ysr[:, 0, f, :].bitcast(F32), ALU.subtract)\
                            .then_inc(ysr_ready, 1)
                elif s[0] == "weights":
                    i = s[1]
                    dve.wait_ge(loaded["w"], 16 * 5)
                    if i >= 2:
                        dve.wait_ge(wsum_ready, i - 1)
                    v.tensor_scalar(wbits[:, i % 2], w[:, i * SEG:(i + 1) * SEG].bitcast(I32), LOST_BITS, None,
                                    ALU.bitwise_and).then_inc(wbits_ready, 1)
                elif s[0] == "sumend":
                    head_sum()
                elif s[0] == "spec":
                    src = full(dve, s)
                    re, im = src[:, 0:FB * P], src[:, FB * P:]
                    v.tensor_copy(spec_a[:], re.rearrange("p (f e) -> p f e", f=FB)).then_inc(spec_ready, 1)
                    v.tensor_scalar(spec_b[:, 0, :], im[:, 0:P], mask[:, 0:1], None, ALU.mult).then_inc(spec_ready, 1)
                    v.tensor_copy(spec_b[:, 1, :], im[:, P:]).then_inc(spec_ready, 1)
                    ins = v.tensor_scalar(spec_t[:], im[:, 0:P], mask[:, 1:2], None, ALU.mult)
                    ins.then_inc(spec_ready, 1)
                    dve.wait_ge(spec_ready, 4)
                    v.scalar_tensor_tensor(out=spec_c[:], in0=spec_a[:, 0, :], scalar=mask[:, 0:1], in1=spec_t[:],
                                           op0=ALU.mult, op1=ALU.add).then_inc(spec_ready, 1)
                elif s[0] == "qkv":
                    _, g, t = s
                    if (g, t) == (0, 0):
                        dve.wait_ge(loaded["bqkv"], 16)
                    src = full(dve, s)
                    ins = v.tensor_tensor(tok[:, g * TPG + t, :, :], src[:, 0:3 * P].rearrange("p (s e) -> p s e", s=3),
                                          bqkv[:].rearrange("p (s e) -> p s e", s=3), ALU.add)
                    ins.then_inc(qkv_ready, 1)
                elif s[0] == "fwd":
                    _, g, fb = s
                    xr, xi = full(dve, s + ("re",)), full(dve, s + ("im",))
                    if g == 0:
                        dve.wait_ge(spec_ready, 5)
                    else:
                        dve.wait_ge(ys_ready, 2 * (FB * (g - 1) + fb + 1))
                    sa, sb_ = spec_a[:, fb, :], spec_b[:, fb, :]
                    sc = spec_c[:] if fb == 0 else spec_a[:, 1, :]
                    for i, (x, coef) in enumerate(((xr, sa), (xi, sb_), (xi, sc), (xr, sb_))):
                        ins = v.tensor_tensor(prod[:, fb, i, :].rearrange("p (b e) -> p b e", b=B),
                                              x.rearrange("p (b e) -> p b e", b=B),
                                              coef.unsqueeze(1).broadcast_to([P, B, P]), ALU.mult)
                        ins.then_inc(prod_ready, 1)
                elif s[0] == "toeplitz":
                    dve.wait_ge(loaded["toep"], 16)
                    dve.wait_ge(loaded["small"], 16 * SMALL)
                    dve.wait_ge(const_ready, 4)
                    for h in range(H):
                        v.scalar_tensor_tensor(out=toep[:, h, 0:P], in0=ident[:], scalar=dcol[:, h:h + 1],
                                               in1=toep[:, h, 0:P], op0=ALU.mult, op1=ALU.add).then_inc(toep_ready, 1)
                elif s[0] == "head":
                    _, g, h = s
                    n = g * H + h
                    src = full(dve, s)
                    if n >= 2:
                        dve.wait_ge(y_ready, n - 1)
                    qs = tok[:, g * TPG:(g + 1) * TPG, 2, h * NH:(h + 1) * NH].unsqueeze(2)\
                        .broadcast_to([P, TPG, NH, NH])
                    v.tensor_tensor(qy[:, n % 2], src.rearrange("p (t m n) -> p t m n", t=TPG, m=NH), qs, ALU.mult)\
                        .then_inc(qy_ready, 1)
                    head_sum()
                    unsummed.append((g, h))
                elif s[0] == "wo":
                    if s[1] % LB == 0:
                        dve.wait_ge(xbo_ready, s[1] // LB + 1)
                    residual_and_stats(s, 0, s[1])
                elif s[0] == "x1tr":
                    c = s[1]
                    normalise()
                    src = full(dve, s)
                    dve.wait_ge(x1h_ready, c + 1)
                    ins = v.tensor_tensor(x1T[:, 1, c % LB, :], src, x1T[:, 0, c % LB, :].bitcast(F32), ALU.subtract)
                    ins.then_inc(x1l_ready, 1)
                elif s[0] == "up":
                    _, c, ob = s
                    n = place[(0, c, ob)]
                    src = full(dve, s + (2,))
                    dve.wait_ge(act_ready, n + 1)
                    r = ring[:, n % RING, :]
                    ins = v.scalar_tensor_tensor(out=r, in0=src, scalar=scales[:, 1, ob:ob + 1], in1=r,
                                                 op0=ALU.mult, op1=ALU.mult)
                    ins.then_inc(gate_ready, 1)
                    low_part()
                    pending.append((0, c, ob))
                elif s[0] == "hid":
                    low_part()
                    normalise()
                    pending.append(s[1:])
                elif s[0] == "down":
                    low_part()
                elif s[0] == "ztr":
                    residual_and_stats(s, 1, s[1])
                elif s[0] == "end":
                    normalise()

        @block.tensor
        def _(pe):
            def into(key):
                b, _, before = bank[key]
                if before:
                    pe.wait_ge(*read(before))
                return psum[:, b, :]

            def done(ins, key):
                ins.then_inc(bank_full[bank[key][0]], 1)

            def attention(s):
                if s[0] == "spec":
                    pe.wait_ge(kk_ready, 1)
                    pe.wait_ge(loaded["dft"], 16)
                    out = into(s)
                    for f in range(2 * FB):
                        for lb in range(LB):
                            ins = nc.tensor.matmul(out[:, f * P:(f + 1) * P], dft[:, lb, f * P:(f + 1) * P],
                                                   kkT[:, lb, :], start=(lb == 0), stop=(lb == LB - 1))
                    done(ins, s)
                elif s[0] == "qkv":
                    _, g, t = s
                    pe.wait_ge(loaded["wqkv"], 16)
                    piece = next(i for i, (lo, hi) in enumerate(XT_PIECES) if lo <= g * TPG + t < hi)
                    pe.wait_ge(loaded[f"xT{piece}"], 16)
                    out = into(s)
                    done(nc.tensor.matmul(out[:, 0:3 * P], xT[:, g * TPG + t, :], wqkv[:], start=True, stop=True), s)
                elif s[0] == "fwd":
                    _, g, fb = s
                    pe.wait_ge((kr0_ready, kr1_ready)[g], LB)
                    pe.wait_ge(dftr_ready, 1)
                    for part, f in (("re", fb), ("im", FB + fb)):
                        out = into(s + (part,))
                        terms = [(dftr[:, i, lb, f * P:(f + 1) * P], kr[:, j, lb * B:(lb + 1) * B, :])
                                 for lb in range(LB) for i, j in PARTS]
                        for i, (wt, xt) in enumerate(terms):
                            ins = nc.tensor.matmul(out, wt, xt, start=(i == 0), stop=(i == len(terms) - 1))
                        done(ins, s + (part,))
                elif s[0] == "inv":
                    _, g, lb = s
                    pe.wait_ge(idftr_ready, 1)
                    pe.wait_ge(ysr_ready, 2 * FB * (g + 1))
                    out = into(s)
                    terms = [(idftr[:, i, f, lb * P:(lb + 1) * P], ysr[:, j, f, :])
                             for f in range(2 * FB) for i, j in PARTS]
                    for i, (wt, xt) in enumerate(terms):
                        ins = nc.tensor.matmul(out, wt, xt, start=(i == 0), stop=(i == len(terms) - 1))
                    done(ins, s)
                elif s[0] == "head":
                    _, g, h = s
                    n = g * H + h
                    pe.wait_ge(toep_ready, H)
                    pe.wait_ge(kv_ready, n + 1)
                    out = into(s)
                    half = B * NH * NH
                    x = kv[:, n % KVR].rearrange("p t m n -> p (t m n)")
                    nc.tensor.matmul(out[:, 0:half], toep[:, h, 0:P], x[:, 0:half], start=True, stop=True)
                    nc.tensor.matmul(out[:, half:], toep[:, h, P:], x[:, 0:half], start=True, stop=False)
                    done(nc.tensor.matmul(out[:, half:], toep[:, h, 0:P], x[:, half:], start=False, stop=True), s)
                elif s[0] == "ytr":
                    c = s[1]
                    pe.wait_ge(y_ready, H * (c // LB + 1))
                    pe.wait_ge(const_ready, 4)
                    out = into(s)
                    for b in range(B):
                        ins = nc.tensor.transpose(out[:, b * P:(b + 1) * P],
                                                  y[:, (c % LB) * B + b].rearrange("p h n -> p (h n)"), ident[:])
                    done(ins, s)
                elif s[0] == "wo":
                    c = s[1]
                    pe.wait_ge(yT_ready, c + 1)
                    pe.wait_ge(loaded["small"], 16 * SMALL)
                    out = into(s)
                    for b in range(B):
                        ins = nc.tensor.matmul(out[:, b * P:(b + 1) * P], yT[:, c % LB, b * P:(b + 1) * P], woT[:],
                                               start=True, stop=True)
                    done(ins, s)
                elif s[0] == "wtest":
                    pe.wait_ge(wsum_ready, NW // SEG)
                    out = into(s)
                    done(nc.tensor.matmul(out[0:1, 0:NW // SEG], ones[:], wsum[:], start=True, stop=True), s)
                elif s[0] == "x1tr":
                    c = s[1]
                    pe.wait_ge(norm_ready, CT * (norm_no(0, c) + 1))
                    out = into(s)
                    for b in range(CT):
                        ins = nc.tensor.transpose(out[:, b * P:(b + 1) * P], tok[:, c * CT + b, 0, :], ident[:])
                    done(ins, s)

            def products(out, pairs, exact):
                todo = [(p, part) for p in pairs for part in (0, 1)]
                for i, ((which, k, ob, x), part) in enumerate(todo):
                    wt, xt = w_of(wr if exact else w, which, k, ob), x(part)
                    if not exact:
                        xt = xt.bitcast(F32)
                    ins = nc.tensor.matmul(out, wt, xt, start=(i == 0), stop=(i == len(todo) - 1))
                return ins

            def feed_forward(s, exact):
                if s[0] == "up":
                    _, c, ob = s
                    pe.wait_ge(x1l_ready, c + 1)
                    for which in (0, 1):
                        key = s + (which + 1,)
                        out = into(key)
                        done(products(out, [(which, 0, ob, lambda p: x1T[:, p, c % LB, :])], exact), key)
                elif s[0] in ("hid", "down"):
                    layer, c = (s[1], s[2]) if s[0] == "hid" else (3, s[1])
                    ob = s[3] if s[0] == "hid" else 0
                    n = hidden_no[(layer - 1, c)] % 3
                    low_parts(pe, place[(layer - 1, c, KB - 1)])
                    out = into(s)
                    pairs = [(layer + 1, k, ob, lambda p, k=k: hidden[:, n, p, k, :]) for k in range(KB)]
                    done(products(out, pairs, exact), s)
                elif s[0] == "ztr":
                    c = s[1]
                    pe.wait_ge(z_ready, c + 1)
                    out = into(s)
                    for b in range(CT):
                        ins = nc.tensor.transpose(out[:, b * P:(b + 1) * P], z[:, b * P:(b + 1) * P], ident[:])
                    done(ins, s)

            start = next(i for i, s in enumerate(steps) if s[0] == "up")
            for s in steps[:start]:
                attention(s)
            pe.wait_ge(wflag_ready, 1)
            flag = pe.value_load(wflag[:, 0:1].bitcast(I32))
            with pe.If(flag == 0):
                for s in steps[start:]:
                    attention(s)
                    feed_forward(s, True)
            with pe.Else():
                for s in steps[start:]:
                    attention(s)
                    feed_forward(s, False)


SMALL = 5
XT_PIECES = ((0, 2), (2, 5), (5, 8), (8, 12), (12, 16))
LOST_BITS = (1 << 12) - 1
PARTS = ((0, 0), (0, 1), (1, 0))


def constants():
    import numpy as np

    n = 2 * L
    pos, f = np.arange(L), np.arange(FB * P)
    ang = 2 * np.pi * np.outer(pos, f) / n
    cos, sin = np.cos(ang), np.sin(ang)
    nyquist = np.cos(np.pi * pos)
    im = -sin
    im[:, 0] = nyquist
    fwd = np.concatenate([cos, im], axis=1)
    back_re = 2 * cos.T / n
    back_re[0] /= 2
    back_im = -2 * sin.T / n
    back_im[0] = nyquist / n
    back = np.concatenate([back_re, back_im])
    mask = np.zeros((P, 2))
    mask[1:, 0] = 1
    mask[0, 1] = 1
    f32 = lambda x: np.ascontiguousarray(x, dtype=np.float32)
    return {
        "dft": f32(fwd.reshape(LB, P, -1).transpose(1, 0, 2)),
        "idft": f32(back.reshape(2 * FB, P, L).transpose(1, 0, 2)),
        "mask": f32(mask),
    }


def kernel(**inputs):
    import numpy as np
    import concourse.bacc as bacc
    from concourse.bass_utils import run_bass_kernel_spmd

    i = {k.replace("L0_", "").replace("attn_", ""): np.asarray(v) for k, v in inputs.items()}
    x = i["u"]
    tiled = x.reshape(G, B, LB, P, D).transpose(0, 2, 3, 1, 4)

    def cols(name):
        wt = i[name].T
        return wt.reshape(-1, P, wt.shape[1]).transpose(1, 0, 2).reshape(P, -1)

    padded = np.concatenate([np.zeros((H, P - 1), np.float32), i["ssm_kernel"]], axis=1)

    arrays = constants() | {
        "xT": x.reshape(G, B, LB, P, D).transpose(4, 0, 2, 1, 3).reshape(D, TILES, P),
        "x": tiled.reshape(CHUNKS, P, CT, D),
        "wqkv": np.concatenate([i["Wk"].T, i["Wv"].T, i["Wq"].T], axis=1),
        "bqkv": np.concatenate([i["bk"], i["bv"], i["bq"]]),
        "kkT": i["ssm_k_kernel"].T.reshape(LB, P, D).transpose(1, 0, 2),
        "kd": i["ssm_k_D"][None, :],
        "toep": padded[:, P - 1 + np.arange(L)[None] - np.arange(P)[:, None]].transpose(1, 0, 2),
        "dd": i["D"],
        "woT": i["Wo"].T.reshape(NH, H, D).transpose(1, 0, 2).reshape(D, D),
        "bo": i["bo"],
        "w1T": cols("ffn_w1_w"), "w2T": cols("ffn_w2_w"), "h1T": cols("ffn_h1_w"), "h2T": cols("ffn_h2_w"),
        "w3T": cols("ffn_w3_w"),
        "scales": np.stack([i[f"ffn_{n}_s"].reshape(KB, P).T for n in ("w1", "w2", "h1", "h2")], axis=1),
        "s3": i["ffn_w3_s"][:, None],
    }
    arrays = {k: np.ascontiguousarray(v) for k, v in arrays.items()}
    nc = bacc.Bacc("TRN2", target_bir_lowering=False, num_devices=1)
    aps = {k: nc.dram_tensor(f"in_{k}", v.shape, F32, kind="ExternalInput").ap() for k, v in arrays.items()}
    aps["out"] = nc.dram_tensor("out_x", (CHUNKS, P, CT, D), F32, kind="ExternalOutput").ap()
    build(nc, aps)
    r = run_bass_kernel_spmd(nc, [{f"in_{k}": v for k, v in arrays.items()}], core_ids=[0])
    out = r.results[0]["out_x"].reshape(G, LB, P, B, D)
    return np.ascontiguousarray(out.transpose(0, 3, 1, 2, 4)).reshape(BATCH, L, D)
```

```python
from contextlib import ExitStack

import concourse.bass as bass
from concourse import mybir

F32 = mybir.dt.float32
F32R = mybir.dt.float32r
I32 = mybir.dt.int32
ALU = mybir.AluOpType
ACT = mybir.ActivationFunctionType
AX = mybir.AxisListType

P = 128
BATCH, L, D = 8, 256, 128
NH = 8
H = D // NH
QH = H // 4
G, B, LB = 2, 4, L // P
TPG = LB * B
TILES = G * TPG
CHUNKS, CT = G * LB, B
CW = CT * P
HID = 512
KB = HID // P
EPS = 1e-5
UNITS = [(0, 0, CT), (1, 0, CT), (2, 0, CT), (3, 0, CT // 2), (3, CT // 2, CT)]
SEG = 1408
FB = 2
AHEAD = 3
KVR = AHEAD + 1


ORDER = """
    qkv 0 0-1; kk; qkv 0 2-7; xsplit 0; ksplit 0; xsplit 1; spec; isplit; diag 0-2; fwd 0 0-1;
    qkv 1 0-4; diag 3; ysplit 0 0-1; qkv 1 5-6; ksplit 1; toep 0; qkv 1 7; inv 0 0-1; kv 0 0-1;
    wbits 0; kv 0 2; toep 1; kv 0 3; toep 2; fwd 1 0; kv 0 4; fwd 1 1; ysplit 1 0; head 0 0;
    toep 3; head 0 1; ysplit 1 1; head 0 2-4; kv 0 5; wbits 1; inv 1 0; xbo 0; head 0 5-6; wsum 0;
    kv 0 6; wbits 2; inv 1 1; kv 0 7-8; head 0 7; kv 0 9; head 0 8; kv 0 10; head 0 9; kv 0 11;
    head 0 10; wround 0; kv 0 12-13; wsum 1; wround 1-3; wsum 2; head 0 11; wsum 3; kv 0 14-15;
    kv 1 0-1; head 0 12-14; wbits 3; head 0 15; sumend; head 1 0-2; kv 1 2-6; xbo 1; kv 1 7;
    ytr 0-1; wtest; wo 0; head 1 3; wo 1; norm 0 0; rstd 0 0-1; head 1 4-6; kv 1 8-9; x1tr 0;
    kv 1 10; head 1 7; kv 1 11; norm 0 1; kv 1 12; x1tr 1; head 1 8; up 0 0; head 1 9; kv 1 13-14;
    up 0 1; kv 1 15; head 1 10; up 0 2; head 1 11-12; up 0 3; up 1 0; head 1 13-14; up 1 1-2;
    head 1 15; sumend; up 1 3; hid 1 0 0-1; ytr 2-3; hid 1 0 2; wo 2-3; hid 1 0 3; rstd 0 2;
    hid 1 1 0; rstd 0 3; norm 0 2-3; hid 1 1 1-3; hid 2 0 0; x1tr 2-3; hid 2 0 1-3; hid 2 1 0-3;
    up 2 0-3; down 0; up 3 0-3; down 1; rstd 1 0; hid 1 2 0-3; hid 1 3 0-2; rstd 1 1; ztr 0-1;
    norm 1 0-1; hid 1 3 3; hid 2 2 0-3; hid 2 3 0-3; down 2; ztr 2; down 3-4; rstd 1 2; ztr 3-4;
    rstd 1 3-4; norm 1 2-4
"""


def step_order():
    out = []
    for step in ORDER.split(";"):
        kind, *index = step.split()
        lead, last = [int(n) for n in index[:-1]], index[-1:] or [""]
        lo, _, hi = last[0].partition("-")
        if not lo:
            out.append((kind,))
        else:
            out += [(kind, *lead, n) for n in range(int(lo), int(hi or lo) + 1)]
    return out


def banks_of(steps):
    at, used, last, turn = {}, [0] * 8, [None] * 8, {}

    def take(key, pool):
        n = turn.get(pool, 0)
        turn[pool] = n + 1
        bank = pool[n % len(pool)]
        at[key] = (bank, used[bank], last[bank])
        used[bank] += 1
        last[bank] = key

    front, side, every = (0, 1, 2, 3), (4, 5, 6, 7), tuple(range(8))
    heads_done = False
    for s in steps:
        late = every if heads_done else side
        if s[0] == "spec" or s[0] in ("qkv", "inv"):
            take(s, side)
        elif s[0] == "fwd":
            take(s + ("re",), front)
            take(s + ("im",), front)
        elif s[0] == "head":
            take(s, front)
            heads_done = s == ("head", 1, H - 1)
        elif s[0] == "up":
            take(s + (1,), late)
            take(s + (2,), late)
        elif s[0] == "wtest":
            take(s, side)
        elif s[0] in ("ytr", "wo", "x1tr", "hid", "down", "ztr"):
            take(s, late)
    return at


def build(nc, a):
    steps = step_order()
    bank = banks_of(steps)
    blocks = [(0,) + s[1:] if s[0] == "up" else s[1:] for s in steps if s[0] in ("up", "hid")]
    place = {b: n for n, b in enumerate(blocks)}
    layers = sorted({b[:2] for b in blocks}, key=lambda lc: place[lc + (0,)])
    hidden_no = {lc: n for n, lc in enumerate(layers)}
    RING = 4

    with ExitStack() as ctx:
        def sb(name, shape, dt=F32):
            return ctx.enter_context(nc.sbuf_tensor(name, shape, dt))

        def sem(name):
            return ctx.enter_context(nc.semaphore(name))

        tok = sb("tok", [P, TILES, 3, P])
        k2 = sb("k2", [P, G, TPG, P])
        toep = sb("toep", [P, H, L])
        kv = sb("kv", [P, KVR, TPG, NH, NH])
        qy = sb("qy", [P, 2, TPG, NH, NH])
        y = sb("y", [P, TPG, H, NH])
        yT = sb("yT", [P, LB, CW])
        x1T = sb("x1T", [P, 2, LB, CW], F32R)
        NW = (2 + 2 * KB) * HID + KB * P
        z = sb("z", [P, 2, CW])
        ident = sb("ident", [P, P])
        wqkv = sb("wqkv", [P, 3 * P])
        bqkv = sb("bqkv", [P, 3 * P])
        woT = sb("woT", [P, P])
        bo = sb("bo", [P, P])
        dcol = sb("dcol", [P, H])
        kd = sb("kd", [1, P])
        mask = sb("mask", [P, 2])
        scales = sb("scales", [P, 4, KB])
        s3 = sb("s3", [P, 1])
        w = sb("w", [P, NW])
        wbits = sb("wbits", [P, 2, SEG], I32)
        ones = sb("ones", [P, 1])
        halves = sb("halves", [P, CT])
        stats = sb("stats", [P, 2, CHUNKS, CT, nc.vector.BN_STATS_DIM])
        mv = sb("mv", [P, 2, CHUNKS, CT, nc.vector.BN_AGGR_DIM])
        rstd = sb("rstd", [P, 2, CHUNKS, 3, CT])
        wsum = sb("wsum", [P, NW // SEG])
        wflag = sb("wflag", [1, NW // SEG + 1])

        early = ctx.enter_context(ExitStack())

        def esb(name, shape, dt=F32):
            return early.enter_context(nc.sbuf_tensor(name, shape, dt))

        xT = esb("xT", [P, TILES, P])
        dft = esb("dft", [P, LB, 4 * P])
        idft = esb("idft", [P, 2 * FB, L])
        kkT = esb("kkT", [P, LB, P])
        spec_a, spec_b = esb("spec_a", [P, FB, P]), esb("spec_b", [P, FB, P])
        spec_c, spec_t = esb("spec_c", [P, P]), esb("spec_t", [P, P])
        dftr = esb("dftr", [P, 2, LB, 4 * P], F32R)
        idftr = esb("idftr", [P, 2, 2 * FB, L], F32R)
        kr = esb("kr", [P, 2, TPG, P], F32R)
        wqkvr = esb("wqkvr", [P, 2, 3 * P], F32R)
        ysr = esb("ysr", [P, 2, 2 * FB, CW], F32R)
        prod = esb("prod", [P, FB, 4, CW])
        ys = esb("ys", [P, 2 * FB, CW])
        early.close()
        hidden = sb("hidden", [P, 3, 2, KB, CW], F32R)
        ring = sb("ring", [P, RING, CW])
        wr = sb("wr", [P, NW], F32R)

        psum = ctx.enter_context(nc.psum_tensor("psum", [P, 8, 512], F32))

        def w_of(t, which, k, ob):
            if which < 2:
                lo = which * HID + ob * P
            elif which < 4:
                lo = (2 + (which - 2) * KB + k) * HID + ob * P
            else:
                lo = (2 + 2 * KB) * HID + k * P
            return t[:, lo:lo + P]

        loads = ["kk", "dft", "wqkv", "bqkv", "idft", "dd", "toep", "small", "w", "x0", "x1"]
        loads += [f"xT{i}" for i in range(len(XT_PIECES))]
        loaded = {n: sem(f"loaded_{n}") for n in loads}
        bank_full = [sem(f"bank_full{i}") for i in range(8)]
        const_ready = sem("const_ready")
        kk_ready = sem("kk_ready")
        spec_ready = sem("spec_ready")
        spec_c_ready = sem("spec_c_ready")
        qkv_ready = sem("qkv_ready")
        prod_ready = sem("prod_ready")
        ys_ready = sem("ys_ready")
        k2_ready = sem("k2_ready")
        diag_ready = sem("diag_ready")
        toep_ready = sem("toep_ready")
        kv_ready = sem("kv_ready")
        qy_ready = sem("qy_ready")
        y_ready = sem("y_ready")
        split_ready = sem("split_ready")
        dftr_ready = sem("dftr_ready")
        idftr_ready = sem("idftr_ready")
        xh_ready = sem("xh_ready")
        xr_ready = sem("xr_ready")
        kh_ready = sem("kh_ready")
        kr0_ready = sem("kr0_ready")
        kr1_ready = sem("kr1_ready")
        yh_ready = sem("yh_ready")
        ysr_ready = sem("ysr_ready")
        yT_ready = sem("yT_ready")
        xbo_ready = sem("xbo_ready")
        sum_ready = sem("sum_ready")
        stat_ready = sem("stat_ready")
        mv_ready = sem("mv_ready")
        veps_ready = sem("veps_ready")
        rstd_ready = sem("rstd_ready")
        mrs_ready = sem("mrs_ready")
        nmrs_ready = sem("nmrs_ready")
        norm0_ready = sem("norm0_ready")
        norm1_ready = sem("norm1_ready")
        x1h_ready = sem("x1h_ready")
        x1l_ready = sem("x1l_ready")
        act_ready = sem("act_ready")
        gate_ready = sem("gate_ready")
        hi_ready = sem("hi_ready")
        lo_ready = sem("lo_ready")
        lop_ready = sem("lop_ready")
        z_ready = sem("z_ready")
        wr_ready = sem("wr_ready")
        wbits_ready = sem("wbits_ready")
        wsum_ready = sem("wsum_ready")
        wflag_ready = sem("wflag_ready")
        stored = sem("stored")

        def full(eng, key):
            b, n, _ = bank[key]
            eng.wait_ge(bank_full[b], n + 1)
            return psum[:, b, :]

        sums = [(0 if s[0] == "wo" else 1, s[1]) for s in steps if s[0] in ("wo", "ztr")]

        def norm_no(which, u):
            return sums.index((which, u))

        def extent(which, u):
            return UNITS[u] if which else (u, 0, CT)

        def tiles_to(which, u):
            done_ = sums[:norm_no(which, u) + 1]
            return sum(hi - lo for _, lo, hi in (extent(*x) for x in done_))

        def reader_of(layer, c):
            if layer < 2:
                return ("hid", layer + 1, c, KB - 1)
            return ("down", max(u for u, unit in enumerate(UNITS) if unit[0] == c))

        def read(key):
            kind, i = key[0], key[1:]
            if kind == "spec":
                return spec_ready, 5
            if kind == "wtest":
                return wflag_ready, 1
            if kind == "qkv":
                return qkv_ready, i[0] * TPG + i[1] + 1
            if kind == "fwd":
                return prod_ready, 4 * (FB * i[0] + i[1]) + (3 if i[2] == "im" else 4)
            if kind == "inv":
                return k2_ready, i[0] * LB + i[1] + 1
            if kind == "head":
                return qy_ready, i[0] * H + i[1] + 1
            if kind in ("wo", "ztr"):
                return sum_ready, norm_no(int(kind == "ztr"), i[0]) + 1
            if kind == "up" and i[2] == 2:
                return gate_ready, gate_no(i[0], i[1]) + 1
            if kind in ("up", "hid"):
                return act_ready, place[i if kind == "hid" else (0,) + i[:2]] + 1
            return {"ytr": yT_ready, "x1tr": x1l_ready, "down": z_ready}[kind], i[0] + 1

        def pool_makes(b):
            return b[0] == 0 and b[2] % 2 == 1

        def low_parts(eng, n):
            by_pool = sum(map(pool_makes, blocks[:n + 1]))
            if n + 1 > by_pool:
                eng.wait_ge(lo_ready, n + 1 - by_pool)
            if by_pool:
                eng.wait_ge(lop_ready, by_pool)

        def gate_no(c, ob):
            return sum(b[0] == 0 for b in blocks[:place[(0, c, ob)]])

        def diagonals(i):
            if i < 2:
                return qy[:, i].rearrange("p t m n -> p (t m n)").rearrange("p (h l) -> p h l", h=QH)
            half = TPG // 2
            return y[:, (i - 2) * half:(i - 1) * half].rearrange("p t h n -> p (t h n)")\
                .rearrange("p (h l) -> p h l", h=QH)

        def tiles(c):
            return tok[:, c * CT:(c + 1) * CT, 0, :]

        block = ctx.enter_context(nc.Block())

        @block.sync
        def _(sp):
            for i, (lo, hi) in enumerate(XT_PIECES):
                sp.dma_start(xT[:, lo:hi, :], a["xT"][:, lo:hi, :]).then_inc(loaded[f"xT{i}"], 16)
                if i == 1:
                    sp.dma_start(dft[:], a["dft"]).then_inc(loaded["dft"], 16)
                if i == 3:
                    sp.dma_start(idft[:], a["idft"]).then_inc(loaded["idft"], 16)
            sp.dma_start(toep[:], a["toep"]).then_inc(loaded["toep"], 16)
            for t, name in ((woT, "woT"), (scales, "scales"), (s3, "s3")):
                sp.dma_start(t[:], a[name]).then_inc(loaded["small"], 16)
            sp.dma_start(bo[:], a["bo"].partition_broadcast(P)).then_inc(loaded["small"], 16)
            o = 0
            for name in ("w1T", "w2T", "h1T", "h2T", "w3T"):
                n = a[name].shape[1]
                sp.dma_start(w[:, o:o + n], a[name]).then_inc(loaded["w"], 16)
                o += n
            for g in range(G):
                full(sp, ("fwd", g, 1, "im"))
                for c in (2 * g, 2 * g + 1):
                    sp.dma_start(tiles(c), a["x"][c]).then_inc(loaded[f"x{g}"], 16)
            for c, lo, hi in UNITS:
                sp.wait_ge(norm1_ready, CT * c + hi)
                sp.dma_start(a["out"][c][:, lo:hi, :], tiles(c)[:, lo:hi, :]).then_inc(stored, 16)
            sp.wait_ge(stored, 16 * len(UNITS))

        @block.gpsimd
        def _(pool):
            nc.gpsimd.memset(ident[:], 0.0).then_inc(const_ready, 1)
            nc.gpsimd.memset(ones[:], 1.0).then_inc(const_ready, 1)
            nc.gpsimd.memset(halves[:], -0.5).then_inc(const_ready, 1)
            pool.wait_ge(const_ready, 3)
            nc.gpsimd.affine_select(out=ident[:], in_=ident[:], compare_op=ALU.not_equal, fill=1.0, base=0,
                                    pattern=[[-1, P]], channel_multiplier=1).then_inc(const_ready, 1)

            for s in steps:
                if s[0] == "kk":
                    for lb in range(LB):
                        pool.wait_ge(split_ready, lb + 1)
                        nc.gpsimd.tensor_tensor(dftr[:, 1, lb], dft[:, lb], dftr[:, 0, lb].bitcast(F32), ALU.subtract)\
                            .then_inc(dftr_ready, 1)
                elif s[0] == "spec":
                    pool.wait_ge(spec_ready, 5)
                    nc.gpsimd.tensor_tensor(spec_c[:], spec_c[:], spec_t[:], ALU.add).then_inc(spec_c_ready, 1)
                elif s[0] == "isplit":
                    pool.wait_ge(split_ready, LB + 1)
                    nc.gpsimd.tensor_tensor(idftr[:, 1], idft[:], idftr[:, 0].bitcast(F32), ALU.subtract)\
                        .then_inc(idftr_ready, 1)
                elif s[0] == "fwd":
                    _, g, fb = s
                    pool.wait_ge(prod_ready, 4 * (FB * g + fb + 1))
                    if g:
                        pool.wait_ge(ysr_ready, 2 * (FB * (g - 1) + fb + 1))
                    nc.gpsimd.tensor_tensor(ys[:, fb, :], prod[:, fb, 0, :], prod[:, fb, 1, :], ALU.subtract)\
                        .then_inc(ys_ready, 1)
                    nc.gpsimd.tensor_tensor(ys[:, FB + fb, :], prod[:, fb, 2, :], prod[:, fb, 3, :], ALU.add)\
                        .then_inc(ys_ready, 1)
                elif s[0] == "xsplit":
                    if s[1] == 0:
                        pool.wait_ge(xh_ready, 1)
                        nc.gpsimd.tensor_tensor(wqkvr[:, 1], wqkv[:], wqkvr[:, 0].bitcast(F32), ALU.subtract)\
                            .then_inc(xr_ready, 1)
                    pool.wait_ge(xh_ready, s[1] + 2)
                    t = TPG + s[1] * B
                    nc.gpsimd.tensor_tensor(x1T[:, 1, s[1]], xT[:, t:t + B].rearrange("p b l -> p (b l)"),
                                            x1T[:, 0, s[1]].bitcast(F32), ALU.subtract).then_inc(xr_ready, 1)
                elif s == ("ksplit", 1):
                    for lb in range(LB):
                        t = TPG + lb * B
                        pool.wait_ge(kh_ready, LB + lb + 1)
                        nc.gpsimd.tensor_tensor(kr[:, 1, lb * B:(lb + 1) * B, :], tok[:, t:t + B, 0, :],
                                                kr[:, 0, lb * B:(lb + 1) * B, :].bitcast(F32), ALU.subtract)\
                            .then_inc(kr1_ready, 1)
                elif s[0] == "xbo":
                    g = s[1]
                    pool.wait_ge(loaded[f"x{g}"], 16 * LB)
                    pool.wait_ge(loaded["small"], 16 * SMALL)
                    v = tok[:, g * TPG:(g + 1) * TPG, 0, :]
                    nc.gpsimd.tensor_tensor(v, v, bo[:].unsqueeze(1).broadcast_to([P, TPG, P]), ALU.add)\
                        .then_inc(xbo_ready, 1)
                elif s[0] == "kv":
                    _, g, h = s
                    n = g * H + h
                    if h == 0:
                        pool.wait_ge(qkv_ready, TPG * (g + 1))
                        pool.wait_ge(k2_ready, LB * (g + 1))
                    if n >= KVR:
                        full(pool, ("head", (n - KVR) // H, (n - KVR) % H))
                    ks = k2[:, g, :, h * NH:(h + 1) * NH].unsqueeze(2).broadcast_to([P, TPG, NH, NH])
                    vs = tok[:, g * TPG:(g + 1) * TPG, 1, h * NH:(h + 1) * NH].unsqueeze(3)\
                        .broadcast_to([P, TPG, NH, NH])
                    nc.gpsimd.tensor_tensor(kv[:, n % KVR], vs, ks, ALU.mult).then_inc(kv_ready, 1)
                elif s[0] == "up" and pool_makes((0,) + s[1:]):
                    _, c, ob = s
                    n = place[(0, c, ob)]
                    pool.wait_ge(hi_ready, n + 1)
                    h = hidden_no[(0, c)] % 3
                    nc.gpsimd.tensor_tensor(hidden[:, h, 1, ob, :], ring[:, n % RING, :],
                                            hidden[:, h, 0, ob, :].bitcast(F32), ALU.subtract).then_inc(lop_ready, 1)
                elif s[0] == "rstd":
                    _, which, u = s
                    n = norm_no(which, u)
                    c, lo, hi = extent(which, u)
                    veps, rs, mrs = (rstd[:, which, c, j, lo:hi] for j in range(3))
                    pool.wait_ge(mv_ready, tiles_to(which, u))
                    nc.gpsimd.tensor_scalar(veps, mv[:, which, c, lo:hi, 1], EPS, None, ALU.add)\
                        .then_inc(veps_ready, 1)
                    pool.wait_ge(veps_ready, n + 1)
                    nc.gpsimd.tensor_tensor(rs, veps, halves[:, lo:hi], ALU.pow).then_inc(rstd_ready, 1)
                    if which == 0:
                        pool.wait_ge(rstd_ready, n + 1)
                        nc.gpsimd.tensor_tensor(mrs, mv[:, 0, c, :, 0], rs, ALU.mult).then_inc(mrs_ready, 1)

        @block.scalar
        def _(act):
            act.dma_start(wqkv[:], a["wqkv"]).then_inc(loaded["wqkv"], 16)
            act.dma_start(bqkv[:], a["bqkv"].partition_broadcast(P)).then_inc(loaded["bqkv"], 16)
            act.dma_start(kkT[:], a["kkT"]).then_inc(loaded["kk"], 16)
            act.dma_start(kd[:], a["kd"]).then_inc(loaded["kk"], 16)
            act.dma_start(mask[:], a["mask"]).then_inc(loaded["kk"], 16)
            act.dma_start(dcol[:], a["dd"].partition_broadcast(P)).then_inc(loaded["dd"], 16)
            pending = []

            def high_part():
                if not pending:
                    return
                layer, c, ob = b = pending.pop()
                n = place[b]
                if layer == 0:
                    act.wait_ge(gate_ready, gate_no(c, ob) + 1)
                act.wait_ge(act_ready, n + 1)
                h = hidden_no[(layer, c)]
                if h >= 3:
                    full(act, reader_of(*layers[h - 3]))
                nc.scalar.activation(hidden[:, h % 3, 0, ob, :], ring[:, n % RING, :], ACT.Copy)\
                    .then_inc(hi_ready, 1)

            for s in steps:
                if s[0] == "diag":
                    i = s[1]
                    act.wait_ge(loaded["dd"], 16)
                    act.wait_ge(const_ready, 4)
                    for j in range(QH):
                        h = QH * i + j
                        nc.scalar.activation(diagonals(i)[:, j, :], ident[:], ACT.Copy, scale=dcol[:, h:h + 1])\
                            .then_inc(diag_ready, 1)
                elif s[0] == "inv":
                    _, g, lb = s
                    src = full(act, s)
                    ins = nc.scalar.activation(k2[:, g, lb * B:(lb + 1) * B, :],
                                               src.rearrange("p (b e) -> p b e", b=B), ACT.Copy)
                    ins.then_inc(k2_ready, 1)
                elif s[0] == "kk":
                    act.wait_ge(loaded["dft"], 16)
                    for lb in range(LB):
                        nc.scalar.activation(dftr[:, 0, lb], dft[:, lb], ACT.Copy).then_inc(split_ready, 1)
                elif s[0] == "xsplit":
                    if s[1] == 0:
                        act.wait_ge(loaded["wqkv"], 16)
                        nc.scalar.activation(wqkvr[:, 0], wqkv[:], ACT.Copy).then_inc(xh_ready, 1)
                    act.wait_ge(loaded[f"xT{3 + s[1]}"], 16)
                    t = TPG + s[1] * B
                    nc.scalar.activation(x1T[:, 0, s[1]], xT[:, t:t + B].rearrange("p b l -> p (b l)"), ACT.Copy)\
                        .then_inc(xh_ready, 1)
                elif s[0] == "isplit":
                    act.wait_ge(loaded["idft"], 16)
                    nc.scalar.activation(idftr[:, 0], idft[:], ACT.Copy).then_inc(split_ready, 1)
                elif s[0] == "spec":
                    src = full(act, s)
                    re, im = src[:, 0:FB * P], src[:, FB * P:]
                    act.wait_ge(loaded["kk"], 16 * 3)
                    for out, x, scale in ((spec_a[:], re.rearrange("p (f e) -> p f e", f=FB), 1.0),
                                          (spec_b[:, 0, :], im[:, 0:P], mask[:, 0:1]), (spec_b[:, 1, :], im[:, P:], 1.0),
                                          (spec_c[:], re[:, 0:P], mask[:, 0:1]), (spec_t[:], im[:, 0:P], mask[:, 1:2])):
                        nc.scalar.activation(out, x, ACT.Copy, scale=scale).then_inc(spec_ready, 1)
                elif s[0] == "ksplit":
                    g = s[1]
                    for lb in range(LB):
                        t = g * TPG + lb * B
                        act.wait_ge(qkv_ready, t + B)
                        if g:
                            full(act, ("fwd", g - 1, FB - 1, "im"))
                        nc.scalar.activation(kr[:, 0, lb * B:(lb + 1) * B, :], tok[:, t:t + B, 0, :], ACT.Copy)\
                            .then_inc(kh_ready, 1)
                elif s[0] == "ysplit":
                    _, g, fb = s
                    for i, f in enumerate((fb, FB + fb)):
                        act.wait_ge(ys_ready, 2 * (FB * g + fb) + i + 1)
                        if g:
                            full(act, ("inv", g - 1, LB - 1))
                        nc.scalar.activation(ysr[:, 0, f, :], ys[:, f, :], ACT.Copy).then_inc(yh_ready, 1)
                elif s[:2] == ("norm", 0):
                    c = s[2]
                    act.wait_ge(mrs_ready, c + 1)
                    m = rstd[:, 0, c, 2, :]
                    nc.scalar.activation(m, m, ACT.Copy, scale=-1.0).then_inc(nmrs_ready, 1)
                    act.wait_ge(nmrs_ready, c + 1)
                    for i in range(CT):
                        t = tok[:, c * CT + i, 0, :]
                        nc.scalar.activation(t, t, ACT.Identity, bias=m[:, i:i + 1], scale=rstd[:, 0, c, 1, i:i + 1])\
                            .then_inc(norm0_ready, 1)
                elif s[0] == "wround":
                    i = s[1]
                    act.wait_ge(loaded["w"], 16 * 5)
                    full(act, ("inv", 1, LB - 1))
                    nc.scalar.activation(wr[:, i * SEG:(i + 1) * SEG], w[:, i * SEG:(i + 1) * SEG], ACT.Copy)\
                        .then_inc(wr_ready, 1)
                elif s[0] == "wsum":
                    i = s[1]
                    act.wait_ge(wbits_ready, i + 1)
                    nc.scalar.activation(wbits[:, i % 2], wbits[:, i % 2], ACT.Copy, accum_out=wsum[:, i:i + 1])\
                        .then_inc(wsum_ready, 1)
                elif s[0] == "ytr":
                    c = s[1]
                    src = full(act, s)
                    if c >= LB:
                        full(act, ("wo", c - LB))
                    ins = nc.scalar.activation(yT[:, c % LB, :], src, ACT.Copy)
                    ins.then_inc(yT_ready, 1)
                elif s[0] == "x1tr":
                    c = s[1]
                    src = full(act, s)
                    if c >= LB:
                        full(act, ("up", c - LB, KB - 1, 2))
                    nc.scalar.activation(x1T[:, 0, c % LB, :], src, ACT.Copy).then_inc(x1h_ready, 1)
                elif s[0] == "wtest":
                    src = full(act, s)
                    nc.scalar.activation(wflag[:, 1:], src[0:1, 0:NW // SEG], ACT.Copy, accum_out=wflag[:, 0:1])\
                        .then_inc(wflag_ready, 1)
                elif s[0] in ("up", "hid"):
                    if s[0] == "up":
                        _, c, ob = s
                        b, key, func, sc = (0, c, ob), s + (1,), ACT.Silu, scales[:, 0, ob:ob + 1]
                    else:
                        _, layer, c, ob = s
                        b, key, func, sc = (layer, c, ob), s, ACT.Gelu, scales[:, 1 + layer, ob:ob + 1]
                    n = place[b]
                    if n == 0:
                        act.wait_ge(loaded["small"], 16 * SMALL)
                    src = full(act, key)
                    if n >= RING:
                        low_parts(act, n - RING)
                    ins = nc.scalar.activation(ring[:, n % RING, :], src, func, scale=sc)
                    ins.then_inc(act_ready, 1)
                    high_part()
                    pending.append(b)
                elif s[0] == "down":
                    high_part()
                    u = s[1]
                    _, lo, hi = UNITS[u]
                    src = full(act, s)
                    if u > 1:
                        full(act, ("ztr", u - 2))
                    ins = nc.scalar.activation(z[:, u % 2, lo * P:hi * P], src[:, lo * P:hi * P], ACT.Copy,
                                               scale=s3[:, 0:1])
                    ins.then_inc(z_ready, 1)

        @block.vector
        def _(dve):
            v = nc.vector
            pending = []
            unsummed = []

            def low_part():
                if not pending:
                    return
                layer, c, ob = b = pending.pop()
                if pool_makes(b):
                    return
                n = place[b]
                dve.wait_ge(hi_ready, n + 1)
                h = hidden_no[(layer, c)] % 3
                v.tensor_tensor(hidden[:, h, 1, ob, :], ring[:, n % RING, :], hidden[:, h, 0, ob, :].bitcast(F32),
                                ALU.subtract).then_inc(lo_ready, 1)

            def head_sum():
                if not unsummed:
                    return
                g, h = unsummed.pop()
                n = g * H + h
                dve.wait_ge(qy_ready, n + 1)
                if n == 0:
                    dve.wait_ge(toep_ready, 4)
                if g and h == 0:
                    full(dve, ("ytr", LB * g - 1))
                v.tensor_reduce(y[:, :, h, :], qy[:, n % 2], AX.X, ALU.add).then_inc(y_ready, 1)

            def residual_and_stats(key, which, u):
                c, lo, hi = extent(which, u)
                before = tiles_to(which, u) - (hi - lo)
                src = full(dve, key)
                t = tiles(c)[:, lo:hi, :]
                v.tensor_tensor(t, src[:, lo * P:hi * P].rearrange("p (b e) -> p b e", b=hi - lo), t, ALU.add)\
                    .then_inc(sum_ready, 1)
                dve.wait_ge(sum_ready, norm_no(which, u) + 1)
                for i in range(lo, hi):
                    v.bn_stats(stats[:, which, c, i, :], tiles(c)[:, i, :]).then_inc(stat_ready, 1)
                for i in range(lo, hi):
                    dve.wait_ge(stat_ready, before + i - lo + 1)
                    v.bn_aggr(mv[:, which, c, i, :], stats[:, which, c, i, :]).then_inc(mv_ready, 1)

            for s in steps:
                if s[0] == "kk":
                    dve.wait_ge(loaded["kk"], 16 * 3)
                    v.tensor_tensor(kkT[0:1, 0, :], kkT[0:1, 0, :], kd[:], ALU.add).then_inc(kk_ready, 1)
                elif s == ("ksplit", 0):
                    for lb in range(LB):
                        t = lb * B
                        dve.wait_ge(kh_ready, lb + 1)
                        v.tensor_tensor(kr[:, 1, lb * B:(lb + 1) * B, :], tok[:, t:t + B, 0, :],
                                        kr[:, 0, lb * B:(lb + 1) * B, :].bitcast(F32), ALU.subtract)\
                            .then_inc(kr0_ready, 1)
                elif s[0] == "ysplit":
                    _, g, fb = s
                    for i, f in enumerate((fb, FB + fb)):
                        dve.wait_ge(yh_ready, 2 * (FB * g + fb) + i + 1)
                        v.tensor_tensor(ysr[:, 1, f, :], ys[:, f, :], ysr[:, 0, f, :].bitcast(F32), ALU.subtract)\
                            .then_inc(ysr_ready, 1)
                elif s[0] == "wbits":
                    i = s[1]
                    dve.wait_ge(loaded["w"], 16 * 5)
                    if i >= 2:
                        dve.wait_ge(wsum_ready, i - 1)
                    v.tensor_scalar(wbits[:, i % 2], w[:, i * SEG:(i + 1) * SEG].bitcast(I32), LOST_BITS, None,
                                    ALU.bitwise_and).then_inc(wbits_ready, 1)
                elif s[0] == "sumend":
                    head_sum()
                elif s[0] == "qkv":
                    _, g, t = s
                    if (g, t) == (0, 0):
                        dve.wait_ge(loaded["bqkv"], 16)
                    src = full(dve, s)
                    ins = v.tensor_tensor(tok[:, g * TPG + t, :, :], src[:, 0:3 * P].rearrange("p (s e) -> p s e", s=3),
                                          bqkv[:].rearrange("p (s e) -> p s e", s=3), ALU.add)
                    ins.then_inc(qkv_ready, 1)
                elif s[0] == "fwd":
                    _, g, fb = s
                    xr, xi = full(dve, s + ("re",)), full(dve, s + ("im",))
                    if g == 0:
                        dve.wait_ge(spec_ready, 5)
                        dve.wait_ge(spec_c_ready, 1)
                    else:
                        dve.wait_ge(ys_ready, 2 * (FB * (g - 1) + fb + 1))
                    sa, sb_ = spec_a[:, fb, :], spec_b[:, fb, :]
                    sc = spec_c[:] if fb == 0 else spec_a[:, 1, :]
                    for i, (x, coef) in enumerate(((xr, sa), (xi, sb_), (xi, sc), (xr, sb_))):
                        ins = v.tensor_tensor(prod[:, fb, i, :].rearrange("p (b e) -> p b e", b=B),
                                              x.rearrange("p (b e) -> p b e", b=B),
                                              coef.unsqueeze(1).broadcast_to([P, B, P]), ALU.mult)
                        ins.then_inc(prod_ready, 1)
                elif s[0] == "toep":
                    i = s[1]
                    dve.wait_ge(diag_ready, QH * (i + 1))
                    dve.wait_ge(loaded["toep"], 16)
                    t = toep[:, QH * i:QH * (i + 1), 0:P]
                    v.tensor_tensor(t, t, diagonals(i), ALU.add).then_inc(toep_ready, 1)
                elif s[0] == "head":
                    _, g, h = s
                    n = g * H + h
                    src = full(dve, s)
                    if n < 2:
                        dve.wait_ge(toep_ready, n + 1)
                    else:
                        dve.wait_ge(y_ready, n - 1)
                    qs = tok[:, g * TPG:(g + 1) * TPG, 2, h * NH:(h + 1) * NH].unsqueeze(2)\
                        .broadcast_to([P, TPG, NH, NH])
                    v.tensor_tensor(qy[:, n % 2], src.rearrange("p (t m n) -> p t m n", t=TPG, m=NH), qs, ALU.mult)\
                        .then_inc(qy_ready, 1)
                    head_sum()
                    unsummed.append((g, h))
                elif s[0] == "wo":
                    if s[1] % LB == 0:
                        dve.wait_ge(xbo_ready, s[1] // LB + 1)
                    residual_and_stats(s, 0, s[1])
                elif s[0] == "x1tr":
                    c = s[1]
                    src = full(dve, s)
                    dve.wait_ge(x1h_ready, c + 1)
                    ins = v.tensor_tensor(x1T[:, 1, c % LB, :], src, x1T[:, 0, c % LB, :].bitcast(F32), ALU.subtract)
                    ins.then_inc(x1l_ready, 1)
                elif s[0] == "up":
                    _, c, ob = s
                    n = place[(0, c, ob)]
                    src = full(dve, s + (2,))
                    dve.wait_ge(act_ready, n + 1)
                    r = ring[:, n % RING, :]
                    ins = v.scalar_tensor_tensor(out=r, in0=src, scalar=scales[:, 1, ob:ob + 1], in1=r,
                                                 op0=ALU.mult, op1=ALU.mult)
                    ins.then_inc(gate_ready, 1)
                    low_part()
                    pending.append((0, c, ob))
                elif s[0] == "hid":
                    low_part()
                    pending.append(s[1:])
                elif s[0] == "down":
                    low_part()
                elif s[0] == "ztr":
                    residual_and_stats(s, 1, s[1])
                elif s[:2] == ("norm", 1):
                    c, lo, hi = UNITS[s[2]]
                    dve.wait_ge(rstd_ready, norm_no(1, s[2]) + 1)
                    for i in range(lo, hi):
                        t = tok[:, c * CT + i, 0, :]
                        v.tensor_scalar(t, t, mv[:, 1, c, i, 0:1], rstd[:, 1, c, 1, i:i + 1],
                                        ALU.subtract, ALU.mult).then_inc(norm1_ready, 1)

        @block.tensor
        def _(pe):
            def into(key):
                b, _, before = bank[key]
                if before:
                    pe.wait_ge(*read(before))
                return psum[:, b, :]

            def done(ins, key):
                ins.then_inc(bank_full[bank[key][0]], 1)

            def attention(s):
                if s[0] == "spec":
                    pe.wait_ge(kk_ready, 1)
                    pe.wait_ge(loaded["dft"], 16)
                    out = into(s)
                    for f in range(2 * FB):
                        for lb in range(LB):
                            ins = nc.tensor.matmul(out[:, f * P:(f + 1) * P], dft[:, lb, f * P:(f + 1) * P],
                                                   kkT[:, lb, :], start=(lb == 0), stop=(lb == LB - 1))
                    done(ins, s)
                elif s[0] == "qkv":
                    _, g, t = s
                    out = into(s)[:, 0:3 * P]
                    if g == 0:
                        pe.wait_ge(loaded["wqkv"], 16)
                        piece = next(i for i, (lo, hi) in enumerate(XT_PIECES) if lo <= t < hi)
                        pe.wait_ge(loaded[f"xT{piece}"], 16)
                        ins = nc.tensor.matmul(out, xT[:, t, :], wqkv[:], start=True, stop=True)
                    else:
                        pe.wait_ge(xr_ready, t // B + 2)
                        cols = slice(t % B * P, (t % B + 1) * P)
                        for n, (i, j) in enumerate(PARTS):
                            ins = nc.tensor.matmul(out, x1T[:, i, t // B, cols], wqkvr[:, j, :], start=(n == 0),
                                                   stop=(n == len(PARTS) - 1))
                    done(ins, s)
                elif s[0] == "fwd":
                    _, g, fb = s
                    for part, f in (("re", fb), ("im", FB + fb)):
                        out = into(s + (part,))
                        for lb in range(LB):
                            if (fb, part) == (0, "re"):
                                pe.wait_ge((kr0_ready, kr1_ready)[g], lb + 1)
                                pe.wait_ge(dftr_ready, lb + 1)
                            for n, (i, j) in enumerate(PARTS):
                                ins = nc.tensor.matmul(out, dftr[:, i, lb, f * P:(f + 1) * P],
                                                       kr[:, j, lb * B:(lb + 1) * B, :], start=(lb == 0 and n == 0),
                                                       stop=(lb == LB - 1 and n == len(PARTS) - 1))
                        done(ins, s + (part,))
                elif s[0] == "inv":
                    _, g, lb = s
                    pe.wait_ge(idftr_ready, 1)
                    out = into(s)
                    order = [f for fb in range(FB) for f in (fb, FB + fb)]
                    for m, f in enumerate(order):
                        if lb == 0:
                            pe.wait_ge(ysr_ready, 2 * FB * g + m + 1)
                        for n, (i, j) in enumerate(PARTS):
                            ins = nc.tensor.matmul(out, idftr[:, i, f, lb * P:(lb + 1) * P], ysr[:, j, f, :],
                                                   start=(m == 0 and n == 0),
                                                   stop=(m == len(order) - 1 and n == len(PARTS) - 1))
                    done(ins, s)
                elif s[0] == "head":
                    _, g, h = s
                    n = g * H + h
                    pe.wait_ge(toep_ready, h // QH + 1)
                    pe.wait_ge(kv_ready, n + 1)
                    out = into(s)
                    half = B * NH * NH
                    x = kv[:, n % KVR].rearrange("p t m n -> p (t m n)")
                    nc.tensor.matmul(out[:, 0:half], toep[:, h, 0:P], x[:, 0:half], start=True, stop=True)
                    nc.tensor.matmul(out[:, half:], toep[:, h, P:], x[:, 0:half], start=True, stop=False)
                    done(nc.tensor.matmul(out[:, half:], toep[:, h, 0:P], x[:, half:], start=False, stop=True), s)
                elif s[0] == "ytr":
                    c = s[1]
                    pe.wait_ge(y_ready, H * (c // LB + 1))
                    pe.wait_ge(const_ready, 4)
                    out = into(s)
                    for b in range(B):
                        ins = nc.tensor.transpose(out[:, b * P:(b + 1) * P],
                                                  y[:, (c % LB) * B + b].rearrange("p h n -> p (h n)"), ident[:])
                    done(ins, s)
                elif s[0] == "wo":
                    c = s[1]
                    pe.wait_ge(yT_ready, c + 1)
                    pe.wait_ge(loaded["small"], 16 * SMALL)
                    out = into(s)
                    for b in range(B):
                        ins = nc.tensor.matmul(out[:, b * P:(b + 1) * P], yT[:, c % LB, b * P:(b + 1) * P], woT[:],
                                               start=True, stop=True)
                    done(ins, s)
                elif s[0] == "wtest":
                    pe.wait_ge(wsum_ready, NW // SEG)
                    out = into(s)
                    done(nc.tensor.matmul(out[0:1, 0:NW // SEG], ones[:], wsum[:], start=True, stop=True), s)
                elif s[0] == "x1tr":
                    c = s[1]
                    out = into(s)
                    for b in range(CT):
                        pe.wait_ge(norm0_ready, CT * c + b + 1)
                        ins = nc.tensor.transpose(out[:, b * P:(b + 1) * P], tok[:, c * CT + b, 0, :], ident[:])
                    done(ins, s)

            def products(out, pairs, exact, waits=()):
                todo = [(p, part) for p in pairs for part in (0, 1)]
                for i, ((which, k, ob, x), part) in enumerate(todo):
                    if waits and part == 0:
                        low_parts(pe, waits[k])
                    wt, xt = w_of(wr if exact else w, which, k, ob), x(part)
                    if not exact:
                        xt = xt.bitcast(F32)
                    ins = nc.tensor.matmul(out, wt, xt, start=(i == 0), stop=(i == len(todo) - 1))
                return ins

            def feed_forward(s, exact):
                if s[0] == "up":
                    _, c, ob = s
                    pe.wait_ge(x1l_ready, c + 1)
                    for which in (0, 1):
                        key = s + (which + 1,)
                        out = into(key)
                        done(products(out, [(which, 0, ob, lambda p: x1T[:, p, c % LB, :])], exact), key)
                elif s[0] in ("hid", "down"):
                    layer, c = (s[1], s[2]) if s[0] == "hid" else (3, UNITS[s[1]][0])
                    ob = s[3] if s[0] == "hid" else 0
                    cut = slice(0, CW) if s[0] == "hid" else slice(UNITS[s[1]][1] * P, UNITS[s[1]][2] * P)
                    n = hidden_no[(layer - 1, c)] % 3
                    out = into(s)
                    pairs = [(layer + 1, k, ob, lambda p, k=k: hidden[:, n, p, k, cut]) for k in range(KB)]
                    waits = [place[(layer - 1, c, k)] for k in range(KB)] if ob == 0 else []
                    done(products(out[:, cut], pairs, exact, waits), s)
                elif s[0] == "ztr":
                    u = s[1]
                    pe.wait_ge(z_ready, u + 1)
                    out = into(s)
                    for b in range(*UNITS[u][1:]):
                        ins = nc.tensor.transpose(out[:, b * P:(b + 1) * P], z[:, u % 2, b * P:(b + 1) * P], ident[:])
                    done(ins, s)

            start = next(i for i, s in enumerate(steps) if s[0] == "up")
            for s in steps[:start]:
                attention(s)
            pe.wait_ge(wr_ready, NW // SEG)
            pe.wait_ge(wflag_ready, 1)
            flag = pe.value_load(wflag[:, 0:1].bitcast(I32))
            with pe.If(flag == 0):
                for s in steps[start:]:
                    attention(s)
                    feed_forward(s, True)
            with pe.Else():
                for s in steps[start:]:
                    attention(s)
                    feed_forward(s, False)


SMALL = 4
XT_PIECES = ((0, 2), (2, 5), (5, 8), (8, 12), (12, 16))
LOST_BITS = (1 << 12) - 1
PARTS = ((0, 0), (0, 1), (1, 0))


def constants():
    import numpy as np

    n = 2 * L
    pos, f = np.arange(L), np.arange(FB * P)
    ang = 2 * np.pi * np.outer(pos, f) / n
    cos, sin = np.cos(ang), np.sin(ang)
    nyquist = np.cos(np.pi * pos)
    im = -sin
    im[:, 0] = nyquist
    fwd = np.concatenate([cos, im], axis=1)
    back_re = 2 * cos.T / n
    back_re[0] /= 2
    back_im = -2 * sin.T / n
    back_im[0] = nyquist / n
    back = np.concatenate([back_re, back_im])
    mask = np.zeros((P, 2))
    mask[1:, 0] = 1
    mask[0, 1] = 1
    f32 = lambda x: np.ascontiguousarray(x, dtype=np.float32)
    return {
        "dft": f32(fwd.reshape(LB, P, -1).transpose(1, 0, 2)),
        "idft": f32(back.reshape(2 * FB, P, L).transpose(1, 0, 2)),
        "mask": f32(mask),
    }


def kernel(**inputs):
    import numpy as np
    import concourse.bacc as bacc
    from concourse.bass_utils import run_bass_kernel_spmd

    i = {k.replace("L0_", "").replace("attn_", ""): np.asarray(v) for k, v in inputs.items()}
    x = i["u"]
    tiled = x.reshape(G, B, LB, P, D).transpose(0, 2, 3, 1, 4)

    def cols(name):
        wt = i[name].T
        return wt.reshape(-1, P, wt.shape[1]).transpose(1, 0, 2).reshape(P, -1)

    padded = np.concatenate([np.zeros((H, P - 1), np.float32), i["ssm_kernel"]], axis=1)

    arrays = constants() | {
        "xT": x.reshape(G, B, LB, P, D).transpose(4, 0, 2, 1, 3).reshape(D, TILES, P),
        "x": tiled.reshape(CHUNKS, P, CT, D),
        "wqkv": np.concatenate([i["Wk"].T, i["Wv"].T, i["Wq"].T], axis=1),
        "bqkv": np.concatenate([i["bk"], i["bv"], i["bq"]]),
        "kkT": i["ssm_k_kernel"].T.reshape(LB, P, D).transpose(1, 0, 2),
        "kd": i["ssm_k_D"][None, :],
        "toep": padded[:, P - 1 + np.arange(L)[None] - np.arange(P)[:, None]].transpose(1, 0, 2),
        "dd": i["D"],
        "woT": i["Wo"].T.reshape(NH, H, D).transpose(1, 0, 2).reshape(D, D),
        "bo": i["bo"],
        "w1T": cols("ffn_w1_w"), "w2T": cols("ffn_w2_w"), "h1T": cols("ffn_h1_w"), "h2T": cols("ffn_h2_w"),
        "w3T": cols("ffn_w3_w"),
        "scales": np.stack([i[f"ffn_{n}_s"].reshape(KB, P).T for n in ("w1", "w2", "h1", "h2")], axis=1),
        "s3": i["ffn_w3_s"][:, None],
    }
    arrays = {k: np.ascontiguousarray(v) for k, v in arrays.items()}
    nc = bacc.Bacc("TRN2", target_bir_lowering=False, num_devices=1)
    aps = {k: nc.dram_tensor(f"in_{k}", v.shape, F32, kind="ExternalInput").ap() for k, v in arrays.items()}
    aps["out"] = nc.dram_tensor("out_x", (CHUNKS, P, CT, D), F32, kind="ExternalOutput").ap()
    build(nc, aps)
    r = run_bass_kernel_spmd(nc, [{f"in_{k}": v for k, v in arrays.items()}], core_ids=[0])
    out = r.results[0]["out_x"].reshape(G, LB, P, B, D)
    return np.ascontiguousarray(out.transpose(0, 3, 1, 2, 4)).reshape(BATCH, L, D)
```
